# Optimizing a Trainium2 kernel written in Bass

```python
import numpy as np
import jax
import jax.numpy as jnp

def _softmax(x, axis=-1):
    return jax.nn.softmax(x, axis=axis)

def _gelu(x):
    return jax.nn.gelu(x, approximate=True)

def _silu(x):
    return jax.nn.silu(x)

def _sigmoid(x):
    return jax.nn.sigmoid(x)

def _layernorm(x, axis=-1, eps=1e-05):
    m = jnp.mean(x, axis=axis, keepdims=True)
    v = jnp.var(x, axis=axis, keepdims=True)
    return (x - m) / jnp.sqrt(v + eps)

def _scatter_add(tgt, idx, src, axis=0):
    return tgt.at[idx].add(src)

def _segment_sum(src, seg, n):
    return jax.ops.segment_sum(src, seg, n)
kernel_name = 'mk_flamingo_gated_d2_seqx_r4_828e58'

def setup_inputs(seed: int=0):
    np.random.seed(seed)
    _w = jnp.asarray

    def _rec_inputs():
        import jax
        import jax.numpy as jnp
        _rk = jax.random.key(seed)
        x = 0.0002417 + 0.9998 * jax.random.normal(jax.random.fold_in(_rk, 1), (4, 1024, 256), jnp.float32)
        _lenS = 1024 - jax.random.randint(jax.random.fold_in(_rk, 7), (4,), 0, max(1, 1024 // 4) + 1, jnp.int32)
        _lenS2 = 77 - jax.random.randint(jax.random.fold_in(_rk, 8), (4,), 0, max(1, 77 // 4) + 1, jnp.int32)
        _ctx_1024P = jax.random.normal(jax.random.fold_in(_rk, 11), (4, 16, 256), jnp.float32)
        _ctx_1024c = jax.random.dirichlet(jax.random.fold_in(_rk, 511), 0.3 * jnp.ones((16,), jnp.float32), (4, 77))
        _ctx_1024t = jnp.einsum('bsk,bkd->bsd', _ctx_1024c, _ctx_1024P)
        _ctx_1024t = _ctx_1024t * jax.lax.rsqrt(jnp.mean(jnp.square(_ctx_1024t)) + 1e-12) * 0.953939
        ctx_1024 = 7.22013e-05 + 1.00017 * (_ctx_1024t + 0.3 * jax.random.normal(jax.random.fold_in(_rk, 611), (4, 77, 256), jnp.float32))
        _validS = jnp.arange(1024)[None, :] < _lenS[:, None]
        _validS2 = jnp.arange(77)[None, :] < _lenS2[:, None]
        _causal = jnp.tril(jnp.ones((1024, 1024), dtype=bool))
        mask_BxS2_ik0 = jnp.where(jnp.broadcast_to(_validS2[:, :], (4, 77)), 0, 1).astype(jnp.int32)
        _g = jax.random.normal(jax.random.fold_in(_rk, 9001), (2, 2), jnp.float32)
        _g = jnp.sign(_g) * jnp.maximum(jnp.abs(_g), 1.0) + (_g == 0) * 1.0
        g_xattn = _g[0]
        g_ffn = _g[1]
        return (x, ctx_1024, mask_BxS2_ik0, g_xattn, g_ffn)
    x, ctx_1024, mask_BxS2_ik0, g_xattn, g_ffn = _rec_inputs()

    def _L0_xattn_setup():
        import jax, jax.numpy as jnp
        import numpy as np
        EMBED = 256
        HEADS = 16
        HEAD_DIM = EMBED // HEADS
        EXP_DIM = 2 * HEAD_DIM

        def _feature_map(x, fm_w, fm_b):
            z = jnp.einsum('nshd,ed->nshe', x, fm_w) + fm_b
            return jnp.concatenate([jnp.exp(z), jnp.exp(-z)], axis=-1)
        key = jax.random.key(seed)
        ks = jax.random.split(key, 7)
        N, S = (4, 512)
        values = jax.random.normal(ks[0], (N, S, EMBED), dtype=jnp.float32)
        keys_ = jax.random.normal(ks[1], (N, S, EMBED), dtype=jnp.float32)
        query = jax.random.normal(ks[2], (N, S, EMBED), dtype=jnp.float32)
        fm_w = jnp.eye(HEAD_DIM, dtype=jnp.float32) + 0.02 * jax.random.normal(ks[3], (HEAD_DIM, HEAD_DIM), dtype=jnp.float32)
        fm_b = 0.02 * jax.random.normal(ks[4], (HEAD_DIM,), dtype=jnp.float32)
        fc_w = jax.random.normal(ks[5], (EMBED, HEADS * EXP_DIM), dtype=jnp.float32) * (1.0 / np.sqrt(HEADS * EXP_DIM))
        fc_b = jnp.zeros((EMBED,), dtype=jnp.float32)
        return {'values': values, 'keys': keys_, 'query': query, 'fm_w': fm_w, 'fm_b': fm_b, 'fc_w': fc_w, 'fc_b': fc_b}
    _L0_xattn_all = _L0_xattn_setup()
    _L0_xattn_in = {k: v for k, v in _L0_xattn_all.items() if k in ('fm_w', 'fm_b', 'fc_w', 'fc_b')}
    del _L0_xattn_all

    def _L0_ffn_setup():
        import jax, jax.numpy as jnp
        import numpy as np
        B, S, H, E = (8, 1024, 256, 8)
        TEMPERATURE = 1.0
        key = jax.random.key(seed)
        ks = jax.random.split(key, 7)
        s_h = 1.0 / np.sqrt(H).astype(np.float32)
        s_h2 = 1.0 / np.sqrt(H // 2).astype(np.float32)
        return {'hidden_states': jax.random.normal(ks[0], (B, S, H), jnp.float32), 'W1': jax.random.normal(ks[1], (H, H // 2), jnp.float32) * s_h, 'b1': jnp.zeros((H // 2,), jnp.float32), 'W2': jax.random.normal(ks[2], (H // 2, E), jnp.float32) * s_h2, 'b2': jnp.zeros((E,), jnp.float32), 'expert_W': jax.random.normal(ks[3], (E, H, H), jnp.float32) * s_h, 'expert_b': jax.random.normal(ks[4], (E, H), jnp.float32)}
    _L0_ffn_all = _L0_ffn_setup()
    _L0_ffn_in = {k: v for k, v in _L0_ffn_all.items() if k in ('W1', 'b1', 'W2', 'b2', 'expert_W', 'expert_b')}
    del _L0_ffn_all

    def _L1_xattn_setup():
        import jax, jax.numpy as jnp
        import numpy as np
        E = 256
        H = 16
        D = E // H
        key = jax.random.key(seed)
        ks = jax.random.split(key, 8)
        B, Lq, Lkv = (2, 512, 512)
        scale = 1.0 / np.sqrt(E)
        return {'query': jax.random.normal(ks[0], (B, Lq, E), dtype=jnp.float32), 'key_value': jax.random.normal(ks[1], (B, Lkv, E), dtype=jnp.float32), 'mask': jax.random.randint(ks[2], (B, Lkv), 0, 2, dtype=jnp.int32), 'Wq': jax.random.normal(ks[3], (E, E), dtype=jnp.float32) * scale, 'bq': jnp.zeros((E,), dtype=jnp.float32), 'Wk': jax.random.normal(ks[4], (E, E), dtype=jnp.float32) * scale, 'bk': jnp.zeros((E,), dtype=jnp.float32), 'Wv': jax.random.normal(ks[5], (E, E), dtype=jnp.float32) * scale, 'bv': jnp.zeros((E,), dtype=jnp.float32), 'Wo': jax.random.normal(ks[6], (E, E), dtype=jnp.float32) * scale, 'bo': jnp.zeros((E,), dtype=jnp.float32)}
    _L1_xattn_all = _L1_xattn_setup()
    _L1_xattn_in = {k: v for k, v in _L1_xattn_all.items() if k in ('Wq', 'bq', 'Wk', 'bk', 'Wv', 'bv', 'Wo', 'bo')}
    del _L1_xattn_all

    def _L1_ffn_setup():
        import jax, jax.numpy as jnp
        import numpy as np
        K = 4
        ROUTED_SCALING = 1.0
        NORM_TOPK = True

        def _gate(hidden_states, router_w, router_bias):
            logits = jnp.einsum('bsh,he->bse', hidden_states, router_w).astype(jnp.float32)
            scores = jax.nn.softmax(logits, axis=-1)
            corrected = scores + router_bias
            _, top_k_indices = jax.lax.top_k(corrected, K)
            top_k_weights = jnp.take_along_axis(scores, top_k_indices, axis=-1)
            if NORM_TOPK:
                top_k_weights = top_k_weights / (top_k_weights.sum(-1, keepdims=True) + 1e-20)
            top_k_weights = top_k_weights * ROUTED_SCALING
            return (top_k_weights.astype(hidden_states.dtype), top_k_indices)
        key = jax.random.key(seed)
        ks = jax.random.split(key, 9)
        B, S, H, E, I, IS = (2, 256, 256, 8, 128, 512)
        sc = 0.02
        return {'hidden_states': jax.random.normal(ks[0], (B, S, H), jnp.float32), 'router_w': jax.random.normal(ks[1], (H, E), jnp.float32) * sc, 'router_bias': jnp.zeros((), jnp.float32), 'gate_w': jax.random.normal(ks[2], (E, H, I), jnp.float32) * sc, 'up_w': jax.random.normal(ks[3], (E, H, I), jnp.float32) * sc, 'down_w': jax.random.normal(ks[4], (E, I, H), jnp.float32) * sc, 's_gate_w': jax.random.normal(ks[5], (H, IS), jnp.float32) * sc, 's_up_w': jax.random.normal(ks[6], (H, IS), jnp.float32) * sc, 's_down_w': jax.random.normal(ks[7], (IS, H), jnp.float32) * sc}
    _L1_ffn_all = _L1_ffn_setup()
    _L1_ffn_in = {k: v for k, v in _L1_ffn_all.items() if k in ('router_w', 'router_bias', 'gate_w', 'up_w', 'down_w', 's_gate_w', 's_up_w', 's_down_w')}
    del _L1_ffn_all
    return {'x': x, 'ctx_1024': ctx_1024, 'mask_BxS2_ik0': mask_BxS2_ik0, 'g_xattn': g_xattn, 'g_ffn': g_ffn, 'L0_xattn_fm_w': _L0_xattn_in['fm_w'], 'L0_xattn_fm_b': _L0_xattn_in['fm_b'], 'L0_xattn_fc_w': _L0_xattn_in['fc_w'], 'L0_xattn_fc_b': _L0_xattn_in['fc_b'], 'L0_ffn_W1': _L0_ffn_in['W1'], 'L0_ffn_b1': _L0_ffn_in['b1'], 'L0_ffn_W2': _L0_ffn_in['W2'], 'L0_ffn_b2': _L0_ffn_in['b2'], 'L0_ffn_expert_W': _L0_ffn_in['expert_W'], 'L0_ffn_expert_b': _L0_ffn_in['expert_b'], 'L1_xattn_Wq': _L1_xattn_in['Wq'], 'L1_xattn_bq': _L1_xattn_in['bq'], 'L1_xattn_Wk': _L1_xattn_in['Wk'], 'L1_xattn_bk': _L1_xattn_in['bk'], 'L1_xattn_Wv': _L1_xattn_in['Wv'], 'L1_xattn_bv': _L1_xattn_in['bv'], 'L1_xattn_Wo': _L1_xattn_in['Wo'], 'L1_xattn_bo': _L1_xattn_in['bo'], 'L1_ffn_router_w': _L1_ffn_in['router_w'], 'L1_ffn_router_bias': _L1_ffn_in['router_bias'], 'L1_ffn_gate_w': _L1_ffn_in['gate_w'], 'L1_ffn_up_w': _L1_ffn_in['up_w'], 'L1_ffn_down_w': _L1_ffn_in['down_w'], 'L1_ffn_s_gate_w': _L1_ffn_in['s_gate_w'], 'L1_ffn_s_up_w': _L1_ffn_in['s_up_w'], 'L1_ffn_s_down_w': _L1_ffn_in['s_down_w']}

def reference(x, ctx_1024, mask_BxS2_ik0, g_xattn, g_ffn, L0_xattn_fm_w, L0_xattn_fm_b, L0_xattn_fc_w, L0_xattn_fc_b, L0_ffn_W1, L0_ffn_b1, L0_ffn_W2, L0_ffn_b2, L0_ffn_expert_W, L0_ffn_expert_b, L1_xattn_Wq, L1_xattn_bq, L1_xattn_Wk, L1_xattn_bk, L1_xattn_Wv, L1_xattn_bv, L1_xattn_Wo, L1_xattn_bo, L1_ffn_router_w, L1_ffn_router_bias, L1_ffn_gate_w, L1_ffn_up_w, L1_ffn_down_w, L1_ffn_s_gate_w, L1_ffn_s_up_w, L1_ffn_s_down_w):
    import jax
    import jax.numpy as jnp

    def _L0_xattn_ref(values, keys, query, fm_w, fm_b, fc_w, fc_b):
        import jax, jax.numpy as jnp
        import numpy as np
        EMBED = 256
        HEADS = 16
        HEAD_DIM = EMBED // HEADS
        EXP_DIM = 2 * HEAD_DIM

        def _feature_map(x, fm_w, fm_b):
            z = jnp.einsum('nshd,ed->nshe', x, fm_w) + fm_b
            return jnp.concatenate([jnp.exp(z), jnp.exp(-z)], axis=-1)
        N, S, _ = query.shape
        v = values.reshape(N, -1, HEADS, HEAD_DIM)
        k = keys.reshape(N, -1, HEADS, HEAD_DIM)
        q = query.reshape(N, -1, HEADS, HEAD_DIM)
        v, k, q = (_feature_map(x, fm_w, fm_b) for x in (v, k, q))
        scores = jnp.einsum('nqhd,nkhd->nhqk', q, k) / jnp.sqrt(jnp.float32(EMBED))
        attn = jax.nn.softmax(scores, axis=-1)
        out = jnp.einsum('nhql,nlhd->nqhd', attn, v)
        out = out.reshape(N, S, HEADS * EXP_DIM)
        return out @ fc_w.T + fc_b

    def _L0_ffn_ref(hidden_states, W1, b1, W2, b2, expert_W, expert_b):
        import jax, jax.numpy as jnp
        import numpy as np
        B, S, H, E = (8, 1024, 256, 8)
        TEMPERATURE = 1.0
        h = jax.nn.relu(jnp.einsum('bsh,hf->bsf', hidden_states, W1) + b1)
        logits = jnp.einsum('bsf,fe->bse', h, W2) + b2
        probs = jax.nn.softmax(logits / TEMPERATURE, axis=-1)
        sel = jnp.argmax(probs, axis=-1)
        out = jnp.zeros_like(hidden_states)
        for e in range(E):
            mask = (sel == e)[..., None].astype(hidden_states.dtype)
            xe = hidden_states * mask
            ye = jnp.einsum('bsh,hd->bsd', xe, expert_W[e]) + expert_b[e]
            out = out + ye * mask
        return out

    def _L1_xattn_ref(query, key_value, mask, Wq, bq, Wk, bk, Wv, bv, Wo, bo):
        import jax, jax.numpy as jnp
        import numpy as np
        E = 256
        H = 16
        D = E // H
        B, Lq, _ = query.shape
        Lkv = key_value.shape[1]
        Q = (query @ Wq.T + bq).reshape(B, Lq, H, D)
        K = (key_value @ Wk.T + bk).reshape(B, Lkv, H, D)
        V = (key_value @ Wv.T + bv).reshape(B, Lkv, H, D)
        scores = jnp.einsum('bqhd,bkhd->bhqk', Q, K) / jnp.sqrt(jnp.float32(D))
        scores = jnp.where(mask[:, None, None, :] == 0, -jnp.inf, scores)
        probs = jax.nn.softmax(scores, axis=-1)
        context = jnp.einsum('bhqk,bkhd->bqhd', probs, V).reshape(B, Lq, E)
        return context @ Wo.T + bo

    def _L1_ffn_ref(hidden_states, router_w, router_bias, gate_w, up_w, down_w, s_gate_w, s_up_w, s_down_w):
        import jax, jax.numpy as jnp
        import numpy as np
        K = 4
        ROUTED_SCALING = 1.0
        NORM_TOPK = True

        def _gate(hidden_states, router_w, router_bias):
            logits = jnp.einsum('bsh,he->bse', hidden_states, router_w).astype(jnp.float32)
            scores = jax.nn.softmax(logits, axis=-1)
            corrected = scores + router_bias
            _, top_k_indices = jax.lax.top_k(corrected, K)
            top_k_weights = jnp.take_along_axis(scores, top_k_indices, axis=-1)
            if NORM_TOPK:
                top_k_weights = top_k_weights / (top_k_weights.sum(-1, keepdims=True) + 1e-20)
            top_k_weights = top_k_weights * ROUTED_SCALING
            return (top_k_weights.astype(hidden_states.dtype), top_k_indices)
        B, S, H = hidden_states.shape
        tk_w, tk_i = _gate(hidden_states, router_w, router_bias)
        hf = hidden_states.reshape(-1, H)
        tk_w = tk_w.reshape(-1, K)
        tk_i = tk_i.reshape(-1, K)
        gate_all = jnp.einsum('nh,ehi->nei', hf, gate_w)
        up_all = jnp.einsum('nh,ehi->nei', hf, up_w)
        act = jax.nn.silu(gate_all) * up_all
        down_all = jnp.einsum('nei,eih->neh', act, down_w)
        sel = jnp.take_along_axis(down_all, tk_i[:, :, None], axis=1)
        routed = (sel * tk_w[:, :, None]).sum(axis=1).reshape(B, S, H)
        g = jnp.einsum('bsh,hm->bsm', hidden_states, s_gate_w)
        u = jnp.einsum('bsh,hm->bsm', hidden_states, s_up_w)
        shared = jnp.einsum('bsm,mh->bsh', jax.nn.silu(g) * u, s_down_w)
        return routed + shared
    x = x + jnp.tanh(g_xattn[0]) * _L0_xattn_ref(ctx_1024, ctx_1024, _layernorm(x, axis=-1), L0_xattn_fm_w, L0_xattn_fm_b, L0_xattn_fc_w, L0_xattn_fc_b)
    x = x + jnp.tanh(g_ffn[0]) * _L0_ffn_ref(_layernorm(x, axis=-1), L0_ffn_W1, L0_ffn_b1, L0_ffn_W2, L0_ffn_b2, L0_ffn_expert_W, L0_ffn_expert_b)
    x = x + jnp.tanh(g_xattn[1]) * _L1_xattn_ref(_layernorm(x, axis=-1), ctx_1024, mask_BxS2_ik0, L1_xattn_Wq, L1_xattn_bq, L1_xattn_Wk, L1_xattn_bk, L1_xattn_Wv, L1_xattn_bv, L1_xattn_Wo, L1_xattn_bo)
    x = x + jnp.tanh(g_ffn[1]) * _L1_ffn_ref(_layernorm(x, axis=-1), L1_ffn_router_w, L1_ffn_router_bias, L1_ffn_gate_w, L1_ffn_up_w, L1_ffn_down_w, L1_ffn_s_gate_w, L1_ffn_s_up_w, L1_ffn_s_down_w)
    return x

_drawn_inputs = setup_inputs


def setup_inputs(seed=0):
    import zlib

    import numpy as np

    out = dict(_drawn_inputs(seed))
    spreads = {'g_ffn': (-1.0, 0.6),
     'L0_xattn_fc_b': (0.0, 0.287),
     'L0_ffn_b1': (0.0, 0.1),
     'L0_ffn_b2': (0.0, 0.1),
     'L1_xattn_bq': (0.0, 0.8),
     'L1_xattn_bk': (0.0, 0.8),
     'L1_xattn_bv': (0.0, 0.548),
     'L1_xattn_bo': (0.0, 0.533)}
    factors = {'L1_ffn_router_w': 8.0,
     'L1_ffn_gate_w': 8.0,
     'L1_ffn_up_w': 8.0,
     'L1_ffn_down_w': 8.0,
     'L1_ffn_s_gate_w': 8.0,
     'L1_ffn_s_up_w': 8.0,
     'L1_ffn_s_down_w': 8.0}
    for name, (base, spread) in spreads.items():
        noise = np.random.default_rng([zlib.crc32(name.encode()), seed]).standard_normal(out[name].shape)
        drawn = base * np.exp(spread * noise) if base else spread * noise
        out[name] = jnp.asarray(drawn.astype(out[name].dtype))
    for name, factor in factors.items():
        out[name] = (out[name] * factor).astype(out[name].dtype)
    return out
```

```python
from contextlib import ExitStack

import numpy as np

import concourse.bass as bass
from concourse import mybir

F32 = mybir.dt.float32
F16 = mybir.dt.float16
I32 = mybir.dt.int32
U32 = mybir.dt.uint32
ALU = mybir.AluOpType
ACT = mybir.ActivationFunctionType
AX = mybir.AxisListType.X

P = 128
D = 256
KC = D // P
B = 4
S = 1024
NK = 77
H = 16
TB = 256
SUB = TB // P
NB = B * S // TB
BPB = S // TB
HK = H * NK
GW = HK // 4
NCH = (HK + P - 1) // P
HKP = NCH * P
E = 8
TOPK = 4
NI = 128
NSH = 4
WS = 16.0
EPS = 1e-5
FINITE_LOW = -1.0e30

BANKS = ("T0", "T1", "F0", "F1", "S0", "S1")


def att_steps(layer):
    head = [("aL", layer), ("aX", layer), ("aZ", layer)]
    return head


def events(step):
    kind, layer = step[0], step[1]
    if kind == "aL":
        return {"a_stats": 1, "a_rstd": 1, "a_xn": 1, "a_xb": 1}
    if kind == "aX":
        return {"T0": 1, "a_xh": 1}
    if kind == "aZ":
        return {"T1": 1, "T0": 1} if layer == 0 else {"T1": 1}
    if kind == "aS":
        return {f"S{step[2] % 2}": 1, "a_d": 1, "a_exp": 1}
    if kind == "aN":
        return {"a_rs": 1, "a_pn": 1}
    if kind == "aT":
        return {"T1": 2, "T0": 1}
    if kind == "aO":
        return {"T0": 1}
    if kind == "fL":
        return {"f_stats": 1, "f_rstd": 1, "f_xn": 1}
    if kind == "fX":
        return {"T1": 1, "f_xh": 1}
    if kind == "fH":
        return {"T0": 1, "f_hs": 1}
    if kind == "fM":
        return {"T1": 1, "f_mask": 1}
    if kind == "fB":
        return {"T0": 1, "T1": 1}
    if kind == "fE":
        return {f"F{step[3] % 2}": 1}
    if kind == "fR":
        return {"T0": 1, "f_nmx": 1, "f_re": 1}
    if kind == "fG":
        return {f"F{step[2] % 2}": 1, "f_th": 1}
    if kind == "fA":
        return {"f_b": 1, "f_ah": 1, "f_act": 1}
    if kind == "fD":
        return {"T1": 1}
    if kind == "pF":
        return {"T0": 2, "T1": 2}
    if kind == "pW":
        return {"T0": NCH // 2, "T1": NCH // 2, "p_kv": 1}
    raise ValueError(kind)


def block_steps(att, ffn):
    a = {}
    if att is not None:
        a = {k: ("aS", att, k) for k in range(4)}
    if ffn == 0:
        head = [("fL", 0), ("fX", 0), ("fH", 0), ("fM", 0, 0), ("fM", 0, 1)]
        body = [("fE", 0, s, p) for p in range(E // 2) for s in range(SUB)]
        body = body[:2] + [("fB", 0, 0), ("fB", 0, 1)] + body[2:]
        per = 3
    elif ffn == 1:
        head = [("fL", 1), ("fX", 1), ("fR", 1, 0), ("fR", 1, 1)]
        body = []
        nj = E + NSH
        for j in range(nj + 2):
            if j < nj:
                body.append(("fG", 1, j))
            if 1 <= j <= nj:
                body.append(("fA", 1, j - 1))
            if 2 <= j and j - 2 < E:
                body.append(("fD", 1, j - 2))
        body.append(("fD", 1, E))
        per = 8
    else:
        head, body, per = [], [], 0
    if att is None:
        return head + body
    out = [("aL", att)]
    if ffn is not None:
        out += head[:1]
    out += [("aX", att)]
    if ffn is not None:
        out += head[1:2]
    out += [("aZ", att)]
    out += head[2:]
    body = list(body)

    def fill(n):
        take, body[:] = body[:n], body[n:]
        return take

    out += [a[0], a[1]]
    out += fill(per)
    out += [("aN", att, 0), a[2]] + fill(per // 2) + [("aN", att, 1), a[3]] + fill(per // 2)
    out += [("aT", att, 0)] + fill(1) + [("aO", att, 0), ("aN", att, 2)] + fill(per)
    out += [("aN", att, 3)] + fill(per // 2) + [("aT", att, 1)] + fill(1) + [("aO", att, 1)]
    return out + body


class Tally:

    def __init__(self):
        self.n, self.rate, self.it = {}, {}, None

    def past(self, name, more=0):
        n = self.n.get(name, 0) + more
        if self.it is None:
            return n
        return self.it * self.rate.get(name, 0) + n

    def step(self, names):
        for k, v in names.items():
            self.n[k] = self.n.get(k, 0) + v

    def enter(self, it, rate):
        self.it, self.rate = it, rate

    def leave(self, trips):
        self.it = None
        for k, v in self.rate.items():
            self.n[k] = self.n.get(k, 0) + v * (trips - 1)


class Dry:

    def __getattr__(self, name):
        return lambda *a, **k: self


def gated_layers(nc, a):
    with ExitStack() as ctx:
        def sb(name, shape, dt=F32):
            return ctx.enter_context(nc.sbuf_tensor(name, shape, dt))

        def pb(name, shape):
            return ctx.enter_context(nc.psum_tensor(name, shape, F32))

        x_sb = sb("x_sb", [P, NB * SUB, D])
        ctx_t = sb("ctx_t", [P, KC, B * NK])
        fo_w = sb("fo_w", [P, 4, D])
        k_bd = sb("k_bd", [P, B, HK])
        w_vo = sb("w_vo", [P, B, NCH, D])
        stage = w_vo[:, 2:4, :, :].rearrange("p b c d -> p (b c d)")[:, 0:4096].rearrange(
            "p (a n) -> p a n", a=2)
        probs = sb("probs", [P, SUB, HKP])
        probs_t = sb("probs_t", [P, NCH, P])
        q_t = sb("q_t", [P, 4, TB])
        mv = sb("mv", [P, 2, SUB, 2])
        stats = sb("stats", [P, 2, SUB, 6])
        rstd = sb("rstd", [P, 2, SUB])
        xn = sb("xn", [P, 2, SUB, D])
        kv_w = xn
        xh = sb("xh", [P, 2, KC, TB], F16)
        xl = sb("xl", [P, 2, KC, TB], F16)
        row_max = sb("row_max", [P, 2, 8])
        row_inv = sb("row_inv", [P, 2, 2, 8])
        h_hi = sb("h_hi", [P, TB], F16)
        h_lo = sb("h_lo", [P, TB], F16)
        one_hot = sb("one_hot", [P, SUB, P], F16)
        one_hot_t = sb("one_hot_t", [P, P], F16)
        gate = sb("gate", [P, SUB, E])
        small = sb("small", [P, 12, 8])
        idx = sb("idx", [P, 8], U32)
        th = sb("th", [P, 2, TB])
        h_t = th[:, 0, :]
        act_f = sb("act_f", [P, 2, TB])
        act = sb("act", [P, 2, E + NSH, TB], F16)
        padded = act[:, :, :, :].rearrange("p a j t -> p (a j t)").bitcast(F32)
        feat = probs[:, :, :].rearrange("p s c -> p (s c)")[:, 0:4 * B * NK].rearrange(
            "p (g c) -> p g c", g=4)
        zw32 = sb("zw32", [P, 2, P])
        msk = sb("msk", [P, B, NK])
        mask_i = msk[:, :, :].bitcast(I32)
        x_bias = sb("x_bias", [P, 2, D])
        tg = sb("tg", [P, 4])
        tgw = sb("tgw", [P, 2])
        eps_t = sb("eps_t", [P, SUB])
        rs_exp = sb("rs_exp", [P, SUB])

        consts = {}
        consts["zmask"] = xn[:, 0, 0, :]
        consts["ob"] = q_t[:, 0:2, :].rearrange("p a n -> p (a n)")
        for name, shape in CONSTS.items():
            if name in consts:
                continue
            consts[name] = sb("c_" + name, [P] + list(shape))
        ident, zmask, mask4, mask8, iota8 = (consts[n] for n in ("ident", "zmask", "mask4", "mask8", "iota8"))
        ident16 = sb("ident16", [P, P], F16)

        def split(name, shape):
            return sb(name + "_h", [P] + shape, F16), sb(name + "_l", [P] + shape, F16)

        zw = split("zw", [2, P])
        w1 = split("w1", [KC, P])
        w2 = split("w2", [E])
        ew = split("ew", [KC, E, D])
        eb = split("eb", [D])
        wq = split("wq", [KC, D])
        rw = split("rw", [KC, E])
        gw = split("gw", [KC, E + NSH, NI])
        uw = split("uw", [KC, E + NSH, NI])
        dw = split("dw", [E + NSH, D])

        bank = {n: pb("ps_" + n, [P, 512]) for n in ("T0", "T1", "F0", "F1")}
        bank["S0"] = pb("ps_S0", [P, 2, 512])
        bank["S1"] = pb("ps_S1", [P, 2, 512])

        def sem(name):
            return ctx.enter_context(nc.semaphore(name))

        filled = {n: sem("filled_" + n) for n in BANKS}
        read = {n: sem("read_" + n) for n in BANKS}
        ev = {n: sem(n) for n in (
            "a_stats", "a_rstd", "a_xn", "a_xb", "a_xh", "a_d", "a_exp", "a_rs", "a_pn",
            "f_stats", "f_rstd", "f_xn", "f_xh", "f_hs", "f_mask", "f_nmx", "f_re",
            "f_th", "f_b", "f_ah", "f_act", "p_kv")}
        small_in = sem("small_in")
        x_in = sem("x_in")
        stage_in = [sem("stage_in0"), sem("stage_in1")]
        split_hi = sem("split_hi")
        split_lo = sem("split_lo")
        ready = sem("ready")
        tanh_done = sem("tanh_done")
        fo_in = sem("fo_in")
        out_done = sem("out_done")
        dve_seq = sem("dve_seq")
        pool_seq = sem("pool_seq")

        def part(src, pair, sl):
            return src, sl(pair[0]), sl(pair[1])

        def kcn(w):
            return w.rearrange("(c p) n -> p c n", p=P)

        pieces = [part(kcn(a["L0_ffn_W1"]), w1, lambda t: t[:, :, :]),
                  part(a["L0_ffn_W2"], w2, lambda t: t[:, :])]
        for c in range(KC):
            src = a["L0_ffn_expert_W"].rearrange("e (c p) n -> c p e n", p=P)[c]
            pieces.append(part(src, ew, lambda t, c=c: t[:, c, :, :]))
        pieces += [part(a["expert_b"], eb, lambda t: t[:, :]),
                   part(kcn(a["WqT"]), wq, lambda t: t[:, :, :]),
                   part(kcn(a["L1_ffn_router_w"]), rw, lambda t: t[:, :, :])]
        for nm, sh, w in (("gate_w", "s_gate_w", gw), ("up_w", "s_up_w", uw)):
            for c in range(KC):
                src = a["L1_ffn_" + nm].rearrange("e (c p) n -> c p e n", p=P)[c]
                pieces.append(part(src, w, lambda t, c=c: t[:, c, 0:E, :]))
                src = a["L1_ffn_" + sh].rearrange("(c p) (j n) -> c p j n", p=P, n=NI)[c]
                pieces.append(part(src, w, lambda t, c=c: t[:, c, E:E + NSH, :]))
        pieces.append(part(a["L1_ffn_down_w"].rearrange("e p n -> p e n"), dw, lambda t: t[:, 0:E, :]))
        pieces.append(part(a["L1_ffn_s_down_w"].rearrange("(j p) n -> p j n", p=P), dw,
                           lambda t: t[:, E:E + NSH, :]))

        def staged(k, like):
            n = int(np.prod(like.shape[1:]))
            v = stage[:, k % 2, 0:n]
            if len(like.shape) == 3:
                v = v.rearrange("p (a b) -> p a b", b=like.shape[2])
            return v

        small_loads = [(ctx_t, a["ctxT"].rearrange("(c p) n -> p c n", p=P)),
                       (mask_i, a["mask"])]
        small_loads += [(consts[n], a[n]) for n in CONSTS]

        def prog(walk):
            for layer in range(2):
                prev = 0 if layer == 1 else None
                pre = [("pF", layer)] + [("pW", layer, b) for b in range(B)]
                if prev is not None:
                    walk(pre, None, None)
                    walk(block_steps(layer, prev), 0, NB - 1)
                else:
                    walk(pre, None, None)
                    walk(block_steps(layer, None), 0, None)
                walk(block_steps(layer, layer), 1, 0, trips=NB - 1)
            walk(block_steps(None, 1), None, NB - 1)

        def run(eng, handle, counted=(), after=None):
            t = Tally()

            def walk(steps, ab, fb, trips=None):
                def body(e, i):
                    ablk = ab if i is None or ab is None else i + ab
                    fblk = fb if i is None or fb is None else i + fb
                    for st in steps:
                        handle(e, t, st, ablk if st[0][0] == "a" else fblk)
                        t.step(events(st))
                    if after is not None:
                        after(e, t, steps, fblk)

                if trips is None:
                    body(eng, None)
                    return
                before = dict(t.n)
                body(Dry(), 0)
                rate = {k: v - before.get(k, 0) for k, v in t.n.items()}
                t.n = before
                with eng.Fori(0, trips) as i:
                    t.enter(i, rate)
                    body(eng, i)
                t.leave(trips)

            prog(walk)
            return t

        def at_least(e, s, n):
            if not (isinstance(n, int) and n <= 0):
                e.wait_ge(s, n)

        block = ctx.enter_context(nc.Block())

        @block.sync
        def _(sp):
            for dst, src in small_loads:
                sp.dma_start(dst[tuple([slice(None)] * len(dst.shape))], src).then_inc(small_in, 16)
            sp.dma_start(fo_w[:, :, :], a["fcT"].rearrange("(g p) n -> p g n", p=P)).then_inc(small_in, 16)
            for b in range(B):
                sp.dma_start(x_sb[:, b * 8:(b + 1) * 8, :],
                             a["x"][b].rearrange("(t p) d -> p t d", p=P)).then_inc(x_in, 16)
            for k, (src, hi, _) in enumerate(pieces):
                if k >= 2:
                    sp.wait_ge(split_lo, k - 1)
                np_ = src.shape[0]
                sp.dma_start(staged(k, hi)[0:np_], src).then_inc(stage_in[k % 2], 16)

            def handle(e, t, st, blk):
                if st == ("pF", 1):
                    at_least(e, read["T0"], t.past("T0"))
                    at_least(e, filled["T1"], t.past("T1"))
                    e.dma_start(kv_w[:, 0], kcn(a["WkT"])).then_inc(fo_in, 16)
                    e.dma_start(kv_w[:, 1], kcn(a["WvT"])).then_inc(fo_in, 16)
                    e.dma_start(fo_w[:, 0:KC, :], kcn(a["WoT"])).then_inc(fo_in, 16)

            def store(e, t, steps, fb):
                if ("fD", 1, E) in steps:
                    e.wait_ge(read["T1"], t.past("T1"))
                    dst = a["out"].rearrange("(t p) d -> p t d", p=P)
                    e.dma_start(dst[:, bass.ts(fb, SUB), :],
                                x_sb[:, bass.ts(fb, SUB), :]).then_inc(out_done, 16)

            run(sp, handle, after=store)
            sp.wait_ge(out_done, 16 * NB)

        @block.tensor
        def _(pe):
            def mm3(e, out, lh, ll, rh, rl, first, last):
                e.matmul(out, lh, rh, start=first, stop=False)
                e.matmul(out, lh, rl, start=False, stop=False)
                return e.matmul(out, ll, rh, start=False, stop=last)

            pe.wait_ge(ready, 1)

            def handle(e, t, st, blk):
                kind, layer = st[0], st[1]

                def take(name, use=0):
                    at_least(e, read[name], t.past(name, use))

                if kind == "pF":
                    if layer == 1:
                        e.wait_ge(fo_in, 48)
                    for g in range(4):
                        bk = f"T{g % 2}"
                        take(bk, g // 2)
                        o = bank[bk][:, 0:B * NK]
                        if layer == 0:
                            mm = e.matmul(o, zw32[:, g % 2, :], ctx_t[:, g // 2, :], start=True, stop=True)
                        else:
                            for c in range(KC):
                                mm = e.matmul(o, kv_w[:, g // 2, c, (g % 2) * P:(g % 2) * P + P],
                                              ctx_t[:, c, :], start=(c == 0), stop=(c == KC - 1))
                        mm.then_inc(filled[bk], 1)
                if kind == "pW":
                    e.wait_ge(ev["p_kv"], t.past("p_kv", 1))
                    gw_, ng = (GW, 4) if layer == 0 else (2 * GW, 2)
                    pv = padded[:, 0:ng * (gw_ + 2 * P)].rearrange("p (g c) -> p g c", g=ng)
                    for c in range(NCH):
                        bk = f"T{c % 2}"
                        take(bk, c // 2)
                        gs = [g for g in range(ng) if P * c < gw_ * (g + 1) and P * (c + 1) > gw_ * g]
                        for g in gs:
                            at = P + P * c - gw_ * g
                            mm = e.matmul(bank[bk][:, 0:D], pv[:, g, at:at + P], fo_w[:, g, :],
                                          start=(g == gs[0]), stop=(g == gs[-1]))
                        mm.then_inc(filled[bk], 1)
                if kind in ("aX", "fX"):
                    w = 0 if kind == "aX" else 1
                    bk = "T0" if w == 0 else "T1"
                    e.wait_ge(ev["a_xn" if w == 0 else "f_xn"], t.past("a_xn" if w == 0 else "f_xn"))
                    take(bk)
                    for c in range(KC):
                        for s in range(SUB):
                            mm = e.transpose(bank[bk][:, c * TB + s * P:c * TB + s * P + P],
                                             xn[:, w, s, c * P:c * P + P], ident[:, :])
                    mm.then_inc(filled[bk], 1)
                if kind == "aZ":
                    e.wait_ge(read["T0"], t.past("T0"))
                    for o4 in range(4 if layer == 0 else KC):
                        bk = f"T{1 - o4 // 2}"
                        if o4 % 2 == 0:
                            take(bk)
                        o = bank[bk][:, (o4 % 2) * TB:(o4 % 2) * TB + TB]
                        if layer == 0:
                            mm = mm3(e, o, zw[0][:, o4 % 2, :], zw[1][:, o4 % 2, :],
                                     xh[:, 0, o4 // 2, :], xl[:, 0, o4 // 2, :], True, True)
                        else:
                            for c in range(KC):
                                cols = slice(o4 * P, o4 * P + P)
                                mm = mm3(e, o, wq[0][:, c, cols], wq[1][:, c, cols], xh[:, 0, c, :],
                                         xl[:, 0, c, :], c == 0, c == KC - 1)
                        if o4 % 2 == 1:
                            mm.then_inc(filled[bk], 1)
                if kind == "aS":
                    u = st[2]
                    s, half = u // 2, u % 2
                    bk = f"S{u % 2}"
                    if u == 0:
                        e.wait_ge(read["T1"], t.past("T1"))
                        e.wait_ge(read["T0"], t.past("T0"))
                    take(bk)
                    for gg in range(2):
                        q = (2 * half + gg) if layer == 0 else half
                        at = (2 * half + gg) * GW
                        mm = e.matmul(bank[bk][:, gg, 0:GW], q_t[:, q, s * P:s * P + P],
                                      k_bd[:, blk // BPB, at:at + GW], start=True, stop=True)
                    mm.then_inc(filled[bk], 1)
                if kind == "aT":
                    s = st[2]
                    e.wait_ge(ev["a_pn"], t.past("a_pn"))
                    for piece, bk in enumerate(("T1", "T0", "T1")):
                        take(bk, 1 if piece == 2 else 0)
                        for c in range(4 * piece, min(4 * piece + 4, NCH)):
                            mm = e.transpose(bank[bk][:, (c % 4) * P:(c % 4) * P + P],
                                             probs[:, s, c * P:c * P + P], ident[:, :])
                        mm.then_inc(filled[bk], 1)
                if kind == "aO":
                    e.wait_ge(read["T0"], t.past("T0"))
                    e.wait_ge(read["T1"], t.past("T1"))
                    for c in range(NCH):
                        mm = e.matmul(bank["T0"][:, 0:D], probs_t[:, c, :], w_vo[:, blk // BPB, c, :],
                                      start=(c == 0), stop=(c == NCH - 1))
                    mm.then_inc(filled["T0"], 1)
                if kind == "fH":
                    e.wait_ge(read["T1"], t.past("T1"))
                    take("T0")
                    for c in range(KC):
                        mm = mm3(e, bank["T0"][:, 0:TB], w1[0][:, c, :], w1[1][:, c, :],
                                 xh[:, 1, c, :], xl[:, 1, c, :], c == 0, c == KC - 1)
                    mm.then_inc(filled["T0"], 1)
                if kind == "fM":
                    s = st[2]
                    e.wait_ge(ev["f_hs"], t.past("f_hs"))
                    take("T1")
                    tok = slice(s * P, s * P + P)
                    mm3(e, bank["T1"][:, 0:E], h_hi[:, tok], h_lo[:, tok], w2[0][:, :], w2[1][:, :],
                        True, True).then_inc(filled["T1"], 1)
                if kind == "fB":
                    s = st[2]
                    e.wait_ge(ev["f_mask"], t.past("f_mask"))
                    take("T0")
                    e.transpose(bank["T0"][:, 0:P // 2].bitcast(F16), one_hot[:, s, :],
                                ident16[:, :]).then_inc(filled["T0"], 1)
                    e.wait_ge(read["T0"], t.past("T0", 1))
                    take("T1")
                    e.matmul(bank["T1"][:, 0:D], one_hot_t[:, :], eb[0][:, :], start=True, stop=False)
                    e.matmul(bank["T1"][:, 0:D], one_hot_t[:, :], eb[1][:, :], start=False,
                             stop=True).then_inc(filled["T1"], 1)
                if kind == "fE":
                    s, p2 = st[2], st[3]
                    bk = f"F{p2 % 2}"
                    take(bk)
                    tok = slice(s * P, s * P + P)
                    for c in range(KC):
                        mm = mm3(e, bank[bk][:, :], xh[:, 1, c, tok], xl[:, 1, c, tok],
                                 ew[0][:, c, 2 * p2:2 * p2 + 2, :], ew[1][:, c, 2 * p2:2 * p2 + 2, :],
                                 c == 0, c == KC - 1)
                    mm.then_inc(filled[bk], 1)
                if kind == "fR":
                    s = st[2]
                    e.wait_ge(read["T1"], t.past("T1"))
                    take("T0")
                    tok = slice(s * P, s * P + P)
                    for c in range(KC):
                        mm = mm3(e, bank["T0"][:, 0:E], xh[:, 1, c, tok], xl[:, 1, c, tok],
                                 rw[0][:, c, :], rw[1][:, c, :], c == 0, c == KC - 1)
                    mm.then_inc(filled["T0"], 1)
                if kind == "fG":
                    j = st[2]
                    bk = f"F{j % 2}"
                    take(bk)
                    for m, w in enumerate((gw, uw)):
                        for c in range(KC):
                            mm = mm3(e, bank[bk][:, m * TB:m * TB + TB], w[0][:, c, j, :],
                                     w[1][:, c, j, :], xh[:, 1, c, :], xl[:, 1, c, :],
                                     c == 0, c == KC - 1)
                    mm.then_inc(filled[bk], 1)
                if kind == "fD":
                    j = st[2]
                    js = [j] if j < E else list(range(E, E + NSH))
                    done = js[-1] + 1
                    e.wait_ge(ev["f_act"], t.past("f_act"))
                    take("T1")
                    for s in range(SUB):
                        tok = slice(s * P, s * P + P)
                        for jj in js:
                            mm = mm3(e, bank["T1"][:, s * D:s * D + D], act[:, 0, jj, tok],
                                     act[:, 1, jj, tok], dw[0][:, jj, :], dw[1][:, jj, :],
                                     jj == js[0], jj == js[-1])
                    mm.then_inc(filled["T1"], 1)

            run(pe, handle)

        @block.scalar
        def _(sc):
            sc.wait_ge(small_in, 16 * (len(small_loads) + 1))
            sc.activation(tg[:, :], consts["g_all"][:, :], ACT.Tanh).then_inc(tanh_done, 1)
            for k, (src, hi, _) in enumerate(pieces):
                sc.wait_ge(stage_in[k % 2], 16 * (k // 2 + 1))
                np_ = src.shape[0]
                sc.activation(hi[0:np_], staged(k, hi)[0:np_], ACT.Copy, scale=WS).then_inc(split_hi, 1)

            def handle(e, t, st, blk):
                kind, layer = st[0], st[1]

                def got(name, use=0):
                    e.wait_ge(filled[name], t.past(name, use + 1))

                if kind == "pF":
                    if layer == 0:
                        e.wait_ge(ready, 1)
                    for g in range(4):
                        bk = f"T{g % 2}"
                        got(bk, g // 2)
                        if layer == 0:
                            e.activation(feat[:, g, :], bank[bk][:, 0:B * NK], ACT.Exp,
                                         bias=consts["fm_b"][:, 0:1]).then_inc(read[bk], 1)
                        else:
                            bias = consts["bkv"][:, g:g + 1]
                            e.activation(feat[:, g, :], bank[bk][:, 0:B * NK], ACT.Identity,
                                         bias=bias).then_inc(read[bk], 1)
                if kind == "pW":
                    for c in range(NCH):
                        bk = f"T{c % 2}"
                        got(bk, c // 2)
                        e.activation(w_vo[:, st[2], c, :], bank[bk][:, 0:D], ACT.Copy,
                                     scale=tg[:, layer:layer + 1]).then_inc(read[bk], 1)
                if kind in ("aX", "fX"):
                    w = 0 if kind == "aX" else 1
                    bk = "T0" if w == 0 else "T1"
                    got(bk)
                    e.activation(xh[:, w, :, :], bank[bk][:, :].rearrange("p (c t) -> p c t", c=KC),
                                 ACT.Copy).then_inc(ev["a_xh" if w == 0 else "f_xh"], 1)
                if kind == "aZ":
                    for o2 in range(2 if layer == 0 else 1):
                        bk = f"T{1 - o2}"
                        got(bk)
                        z = bank[bk][:, :].rearrange("p (c t) -> p c t", c=2)
                        if layer == 0:
                            e.activation(q_t[:, 2 * o2:2 * o2 + 2, :], z, ACT.Exp, scale=1.0 / WS,
                                         bias=consts["fm_b"][:, 0:1]).then_inc(read[bk], 1)
                        else:
                            e.activation(q_t[:, 0, :], z[:, 0, :], ACT.Identity, scale=1.0 / WS,
                                         bias=consts["bq"][:, 0:1])
                            e.activation(q_t[:, 1, :], z[:, 1, :], ACT.Identity, scale=1.0 / WS,
                                         bias=consts["bq"][:, 1:2]).then_inc(read[bk], 1)
                if kind == "aS":
                    u = st[2]
                    s, half = u // 2, u % 2
                    e.wait_ge(ev["a_d"], t.past("a_d", 1))
                    v = probs[:, s, half * 2 * GW:(half + 1) * 2 * GW]
                    scale = 1.0 / 16.0 if layer == 0 else 0.25
                    e.activation(v, v, ACT.Exp, scale=scale).then_inc(ev["a_exp"], 1)
                if kind == "aT":
                    for piece, bk in enumerate(("T1", "T0", "T1")):
                        got(bk, 1 if piece == 2 else 0)
                        n = min(4, NCH - 4 * piece)
                        e.activation(probs_t[:, 4 * piece:4 * piece + n, :],
                                     bank[bk][:, 0:n * P].rearrange("p (c t) -> p c t", c=n),
                                     ACT.Copy).then_inc(read[bk], 1)
                if kind == "fH":
                    got("T0")
                    e.activation(h_t, bank["T0"][:, 0:TB], ACT.Relu, scale=1.0 / WS,
                                 bias=consts["b1"][:, 0:1]).then_inc(read["T0"], 1)
                if kind == "fB":
                    got("T0")
                    e.activation(one_hot_t[:, :], bank["T0"][:, 0:P // 2].bitcast(F16),
                                 ACT.Copy).then_inc(read["T0"], 1)
                if kind == "fR":
                    e.wait_ge(ev["f_nmx"], t.past("f_nmx", 1))
                    e.activation(small[:, 2, :], small[:, 0, :], ACT.Exp,
                                 bias=small[:, 1, 0:1]).then_inc(ev["f_re"], 1)
                if kind == "fG":
                    j = st[2]
                    got(f"F{j % 2}")
                    e.activation(th[:, j % 2, :], bank[f"F{j % 2}"][:, 0:TB], ACT.Tanh,
                                 scale=0.5 / WS).then_inc(ev["f_th"], 1)
                if kind == "fA":
                    j = st[2]
                    e.wait_ge(ev["f_b"], t.past("f_b", 1))
                    e.activation(act[:, 0, j, :], act_f[:, j % 2, :], ACT.Copy).then_inc(ev["f_ah"], 1)

            run(sc, handle)

        @block.gpsimd
        def _(pool):
            pool.memset(one_hot[:, :, :], 0.0)
            pool.memset(eb[0][:, :], 0.0)
            pool.memset(eb[1][:, :], 0.0)
            pool.memset(eps_t[:, :], EPS)
            pool.memset(rs_exp[:, :], -0.5).then_inc(pool_seq, 1)
            pool.wait_ge(pool_seq, 1)

            def handle(e, t, st, blk):
                kind, layer = st[0], st[1]

                def link(ins):
                    ins.then_inc(pool_seq, 1)
                    e.wait_ge(pool_seq, t.past("pool_seq", 2))
                    t.step({"pool_seq": 1})

                if kind in ("aL", "fL"):
                    w = 0 if kind == "aL" else 1
                    pre = "a" if w == 0 else "f"
                    e.wait_ge(ev[pre + "_stats"], t.past(pre + "_stats", 1))
                    link(e.tensor_tensor(rstd[:, w, :], mv[:, w, :, 1], eps_t[:, :], ALU.add))
                    e.tensor_tensor(rstd[:, w, :], rstd[:, w, :], rs_exp[:, :],
                                    ALU.pow).then_inc(ev[pre + "_rstd"], 1)
                    if w == 0:
                        e.wait_ge(ev["a_xn"], t.past("a_xn", 1))
                        xs = x_sb[:, bass.ts(blk, SUB), :]
                        e.tensor_tensor(xs, xs, x_bias[:, layer, :].unsqueeze(1).broadcast_to([P, SUB, D]),
                                        ALU.add).then_inc(ev["a_xb"], 1)
                if kind == "aN":
                    u = st[2]
                    s, half = u // 2, u % 2
                    e.wait_ge(ev["a_rs"], t.past("a_rs", 1))
                    v = probs[:, s, half * 2 * GW:(half + 1) * 2 * GW].rearrange("p (h k) -> p h k", k=NK)
                    e.tensor_tensor(v, v, row_inv[:, 1, u % 2, :].unsqueeze(2).broadcast_to([P, 8, NK]),
                                    ALU.mult).then_inc(ev["a_pn"], 1)

            run(pool, handle)

        @block.vector
        def _(dve):
            start = Tally()

            def chain(e, t, ins):
                ins.then_inc(dve_seq, 1)
                e.wait_ge(dve_seq, t.past("dve_seq", 1))
                t.step({"dve_seq": 1})

            dve.wait_ge(small_in, 16 * (len(small_loads) + 1))
            dve.wait_ge(tanh_done, 1)
            dve.wait_ge(pool_seq, 1)
            chain(dve, start, dve.tensor_tensor(
                zw32[:, :, :].rearrange("p a (g e) -> p (a g) e", e=16),
                consts["fm_rep"][:, :].unsqueeze(1).broadcast_to([P, 16, 16]),
                zmask[:, :].rearrange("p (g e) -> p g e", e=16), ALU.mult))
            chain(dve, start, dve.tensor_scalar(zw[0][:, :, :], zw32[:, :, :], WS, None, ALU.mult))
            chain(dve, start, dve.scalar_tensor_tensor(zw[1][:, :, :], zw32[:, :, :], WS, zw[0][:, :, :],
                                                       ALU.mult, ALU.subtract))
            dve.tensor_copy(ident16[:, :], ident[:, :])
            chain(dve, start, dve.tensor_tensor(consts["fm_b"][:, :], consts["fm_b"][:, :],
                                                consts["sign"][:, :], ALU.mult))
            dve.memset(padded[:, :], 0.0)
            chain(dve, start, dve.tensor_scalar(msk[:, :, :], mask_i[:, :, :], 0.0, FINITE_LOW,
                                                ALU.is_equal, ALU.mult))
            dve.tensor_scalar(tgw[:, :], tg[:, 2:4], 1.0 / WS, None, ALU.mult)
            for layer in range(2):
                dve.tensor_scalar(x_bias[:, layer, :], consts["ob"][:, layer * D:layer * D + D],
                                  tg[:, layer:layer + 1], None, ALU.mult)
            chain(dve, start, dve.memset(probs[:, :, HK:HKP], 0.0))
            for k, (src, hi, lo) in enumerate(pieces):
                dve.wait_ge(split_hi, k + 1)
                np_ = src.shape[0]
                dve.scalar_tensor_tensor(lo[0:np_], staged(k, hi)[0:np_], WS, hi[0:np_], ALU.mult,
                                         ALU.subtract).then_inc(split_lo, 1)
            dve.wait_ge(x_in, 16 * B)
            dve.wait_ge(split_lo, len(pieces))
            dve.tensor_copy(small[:, 11, :], iota8[:, :]).then_inc(ready, 1)
            base = start.n["dve_seq"]

            def handle(e, t, st, blk):
                kind, layer = st[0], st[1]

                def link(ins):
                    ins.then_inc(dve_seq, 1)
                    e.wait_ge(dve_seq, t.past("dve_seq", base + 1))
                    t.step({"dve_seq": 1})

                def settle(e):
                    e.tensor_copy(small[:, 11, 0:1], iota8[:, 0:1])

                def got(name, use=0):
                    e.wait_ge(filled[name], t.past(name, use + 1))

                def mine(name, use=0):
                    e.wait_ge(read[name], t.past(name, use + 1))

                if kind == "pW":
                    b = st[2]
                    ng, nh, mk = (4, 4, mask4) if layer == 0 else (2, 8, mask8)
                    gw_ = nh * NK
                    if b == 0:
                        e.wait_ge(read["T0"], t.past("T0"))
                        e.wait_ge(read["T1"], t.past("T1"))
                        if layer == 1:
                            link(e.memset(padded[:, 0:ng * (gw_ + 2 * P)], 0.0))
                    else:
                        e.wait_ge(filled["T1"], t.past("T1"))
                        e.wait_ge(filled["T0"], t.past("T0"))
                    pv = padded[:, 0:ng * (gw_ + 2 * P)].rearrange("p (g c) -> p g c", g=ng)
                    for g in range(ng):
                        head = mk[:, :].unsqueeze(2).broadcast_to([P, nh, NK])
                        kf = feat[:, g, b * NK:b * NK + NK].unsqueeze(1).broadcast_to([P, nh, NK])
                        vf = kf if layer == 0 else feat[:, 2 + g, b * NK:b * NK + NK].unsqueeze(1).broadcast_to(
                            [P, nh, NK])
                        e.tensor_tensor(k_bd[:, b, g * gw_:(g + 1) * gw_].rearrange("p (h k) -> p h k", k=NK),
                                        kf, head, ALU.mult)
                        last = e.tensor_tensor(pv[:, g, P:P + gw_].rearrange("p (h k) -> p h k", k=NK),
                                               vf, head, ALU.mult)
                    last.then_inc(ev["p_kv"], 1)
                if kind in ("aL", "fL"):
                    w = 0 if kind == "aL" else 1
                    pre = "a" if w == 0 else "f"
                    if w == 1:
                        at_least(e, read["T0"], t.past("T0"))
                    else:
                        at_least(e, read["F0"], t.past("F0"))
                        at_least(e, read["F1"], t.past("F1"))
                        at_least(e, read["T1"], t.past("T1"))
                    for s in range(SUB):
                        ins = e.bn_stats(stats[:, w, s, :], x_sb[:, blk * SUB + s, :])
                    link(ins)
                    settle(e)
                    for s in range(SUB):
                        ins = e.bn_aggr(mv[:, w, s, :], stats[:, w, s, :])
                    ins.then_inc(ev[pre + "_stats"], 1)
                    at_least(e, filled["T0"], t.past("T0"))
                    at_least(e, filled["T1"], t.past("T1"))
                    e.wait_ge(ev[pre + "_rstd"], t.past(pre + "_rstd", 1))
                    for s in range(SUB):
                        ins = e.tensor_scalar(xn[:, w, s, :], x_sb[:, blk * SUB + s, :], mv[:, w, s, 0:1],
                                              rstd[:, w, s:s + 1], ALU.subtract, ALU.mult)
                    ins.then_inc(ev[pre + "_xn"], 1)
                if kind in ("aX", "fX"):
                    w = 0 if kind == "aX" else 1
                    bk, evn = ("T0", "a_xh") if w == 0 else ("T1", "f_xh")
                    e.wait_ge(ev[evn], t.past(evn, 1))
                    e.tensor_tensor(xl[:, w, :, :], bank[bk][:, :].rearrange("p (c t) -> p c t", c=KC),
                                    xh[:, w, :, :], ALU.subtract).then_inc(read[bk], 1)
                if kind == "aS":
                    u = st[2]
                    s, half = u // 2, u % 2
                    bk = f"S{u % 2}"
                    got(bk)
                    sc_ = bank[bk][:, :, 0:GW].rearrange("p g (h k) -> p g h k", k=NK)
                    v = probs[:, s, half * 2 * GW:(half + 1) * 2 * GW]
                    v4 = v.rearrange("p (g h k) -> p g h k", g=2, k=NK)
                    m = row_max[:, u % 2, :]
                    if layer == 1:
                        mk = msk[:, blk // BPB, :].unsqueeze(1).unsqueeze(1).broadcast_to([P, 2, 4, NK])
                        e.tensor_tensor(v4, sc_, mk, ALU.add).then_inc(read[bk], 1)
                        mine(bk)
                        sc_ = v4
                    link(e.tensor_reduce(m.rearrange("p (g h) -> p g h", g=2), sc_, AX, ALU.max))
                    mb = m.rearrange("p (g h) -> p g h", g=2).unsqueeze(3).broadcast_to([P, 2, 4, NK])
                    if layer == 0:
                        e.tensor_tensor(v4, sc_, mb, ALU.subtract).then_inc(read[bk], 1)
                        mine(bk)
                        e.tensor_copy(small[:, 10, 0:1], m[:, 0:1]).then_inc(ev["a_d"], 1)
                    else:
                        e.tensor_tensor(v4, sc_, mb, ALU.subtract).then_inc(ev["a_d"], 1)
                if kind == "aN":
                    u = st[2]
                    s, half = u // 2, u % 2
                    e.wait_ge(ev["a_exp"], t.past("a_rs", 1))
                    v = probs[:, s, half * 2 * GW:(half + 1) * 2 * GW].rearrange("p (h k) -> p h k", k=NK)
                    at_least(e, ev["a_pn"], t.past("a_pn", -1))
                    link(e.tensor_reduce(row_inv[:, 0, u % 2, :], v, AX, ALU.add))
                    e.reciprocal(row_inv[:, 1, u % 2, :], row_inv[:, 0, u % 2, :]).then_inc(ev["a_rs"], 1)
                if kind == "aO":
                    s = st[2]
                    got("T0")
                    e.wait_ge(ev["a_xb"], t.past("a_xb"))
                    xs = x_sb[:, blk * SUB + s, :]
                    e.tensor_tensor(xs, bank["T0"][:, 0:D], xs, ALU.add).then_inc(read["T0"], 1)
                if kind == "fH":
                    e.wait_ge(read["T0"], t.past("T0", 1))
                    link(e.tensor_copy(h_hi[:, :], h_t))
                    e.tensor_tensor(h_lo[:, :], h_t, h_hi[:, :], ALU.subtract).then_inc(ev["f_hs"], 1)
                if kind == "fM":
                    s = st[2]
                    got("T1")
                    lg = small[:, 0, :]
                    e.scalar_tensor_tensor(lg, bank["T1"][:, 0:E], 1.0 / WS, consts["b2"][:, :], ALU.mult,
                                           ALU.add).then_inc(read["T1"], 1)
                    mine("T1")
                    settle(e)
                    link(e.max(small[:, 1, :], lg))
                    settle(e)
                    link(e.max_index(idx[:, :], small[:, 1, :], lg))
                    link(e.tensor_copy(small[:, 2, :], idx[:, :]))
                    e.tensor_scalar(gate[:, s, :], iota8[:, :], small[:, 2, 0:1], tgw[:, 0:1],
                                    ALU.is_equal, ALU.mult)
                    e.tensor_scalar(one_hot[:, s, 0:E], iota8[:, :], small[:, 2, 0:1], None,
                                    ALU.is_equal).then_inc(ev["f_mask"], 1)
                if kind == "fB":
                    s = st[2]
                    got("T1")
                    xs = x_sb[:, blk * SUB + s, :]
                    e.wait_ge(read["F0"], t.past("F0"))
                    e.scalar_tensor_tensor(xs, bank["T1"][:, 0:D], tgw[:, 0:1], xs, ALU.mult,
                                           ALU.add).then_inc(read["T1"], 1)
                    mine("T1")
                if kind == "fE":
                    s, p2 = st[2], st[3]
                    bk = f"F{p2 % 2}"
                    got(bk)
                    xs = x_sb[:, blk * SUB + s, :]
                    link(e.scalar_tensor_tensor(xs, bank[bk][:, 0:D], gate[:, s, 2 * p2:2 * p2 + 1], xs,
                                                ALU.mult, ALU.add))
                    e.scalar_tensor_tensor(xs, bank[bk][:, D:2 * D], gate[:, s, 2 * p2 + 1:2 * p2 + 2], xs,
                                           ALU.mult, ALU.add).then_inc(read[bk], 1)
                    mine(bk)
                if kind == "fR":
                    s = st[2]
                    got("T0")
                    e.tensor_scalar(small[:, 0, :], bank["T0"][:, 0:E], 1.0 / WS, None,
                                    ALU.mult).then_inc(read["T0"], 1)
                    mine("T0")
                    settle(e)
                    link(e.max(small[:, 3, :], small[:, 0, :]))
                    e.tensor_scalar(small[:, 1, :], small[:, 3, :], -1.0, None, ALU.mult).then_inc(ev["f_nmx"], 1)
                    e.wait_ge(ev["f_re"], t.past("f_re", 1))
                    link(e.tensor_reduce(small[:, 4, 0:1], small[:, 2, :], AX, ALU.add))
                    link(e.reciprocal(small[:, 4, 1:2], small[:, 4, 0:1]))
                    link(e.tensor_scalar(small[:, 5, :], small[:, 2, :], small[:, 4, 1:2], None, ALU.mult))
                    link(e.tensor_scalar(small[:, 6, :], small[:, 5, :], consts["rb"][:, 0:1], None, ALU.add))
                    settle(e)
                    link(e.max(small[:, 7, :], small[:, 6, :]))
                    settle(e)
                    link(e.max_index(idx[:, :], small[:, 7, :], small[:, 6, :]))
                    link(e.tensor_copy(small[:, 7, :], idx[:, :]))
                    link(e.tensor_scalar(small[:, 8, :], iota8[:, :], small[:, 7, 0:1], None, ALU.is_equal))
                    for k in range(1, TOPK):
                        link(e.scalar_tensor_tensor(small[:, 8, :], iota8[:, :], small[:, 7, k:k + 1],
                                                    small[:, 8, :], ALU.is_equal, ALU.add))
                    link(e.tensor_tensor(small[:, 9, :], small[:, 5, :], small[:, 8, :], ALU.mult))
                    link(e.tensor_reduce(small[:, 4, 2:3], small[:, 9, :], AX, ALU.add))
                    link(e.tensor_scalar(small[:, 4, 3:4], small[:, 4, 2:3], 1e-20, None, ALU.add))
                    link(e.reciprocal(small[:, 4, 4:5], small[:, 4, 3:4]))
                    link(e.tensor_scalar(gate[:, s, :], small[:, 9, :], small[:, 4, 4:5], tgw[:, 1:2],
                                         ALU.mult, ALU.mult))
                if kind == "fA":
                    j = st[2]
                    n = t.past("f_b", 1)
                    bk = f"F{j % 2}"
                    e.wait_ge(ev["f_th"], n)
                    link(e.scalar_tensor_tensor(th[:, j % 2, :], th[:, j % 2, :], 1.0, bank[bk][:, 0:TB],
                                                ALU.add, ALU.mult))
                    e.scalar_tensor_tensor(act_f[:, j % 2, :], th[:, j % 2, :], 0.5 / WS / WS,
                                           bank[bk][:, TB:2 * TB], ALU.mult, ALU.mult).then_inc(ev["f_b"], 1)
                    e.wait_ge(ev["f_b"], n)
                    e.tensor_copy(small[:, 10, 0:1], small[:, 11, 0:1]).then_inc(read[bk], 1)
                    e.wait_ge(ev["f_ah"], n)
                    e.tensor_tensor(act[:, 1, j, :], act_f[:, j % 2, :], act[:, 0, j, :],
                                    ALU.subtract).then_inc(ev["f_act"], 1)
                if kind == "fD":
                    j = st[2]
                    got("T1")
                    for s in range(SUB):
                        xs = x_sb[:, blk * SUB + s, :]
                        g = gate[:, s, j:j + 1] if j < E else tgw[:, 1:2]
                        ins = e.scalar_tensor_tensor(xs, bank["T1"][:, s * D:s * D + D], g, xs,
                                                     ALU.mult, ALU.add)
                    ins.then_inc(read["T1"], 1)
                    mine("T1")

            run(dve, handle)


CONSTS = {"ident": (P,), "zmask": (256,), "mask4": (4,), "mask8": (8,), "iota8": (E,),
          "g_all": (4,), "fm_rep": (16,), "fm_b": (1,), "sign": (1,), "b1": (1,), "b2": (E,), "bq": (KC,),
          "bkv": (2 * KC,), "rb": (1,), "ob": (2 * D,)}


def kernel(**inputs):
    import concourse.bacc as bacc
    from concourse.bass_utils import run_bass_kernel_spmd

    f = {k: np.ascontiguousarray(v) for k, v in inputs.items()}

    def rows(v):
        return np.ascontiguousarray(np.broadcast_to(v.reshape(1, -1), (P, v.size)))

    def cols(v):
        return np.ascontiguousarray(v.reshape(-1, P).T)

    p = np.arange(P)
    zmask = np.zeros((P, 2, 4, 2, 16), np.float32)
    for q in range(P):
        h = q // 16
        zmask[q, h // 4, h % 4, 0, :] = 1.0
        zmask[q, h // 4, h % 4, 1, :] = -1.0
    arrays = {
        "x": f["x"], "ctxT": np.ascontiguousarray(f["ctx_1024"].reshape(B * NK, D).T),
        "WqT": np.ascontiguousarray(f["L1_xattn_Wq"].T), "WkT": np.ascontiguousarray(f["L1_xattn_Wk"].T),
        "WvT": np.ascontiguousarray(f["L1_xattn_Wv"].T), "WoT": np.ascontiguousarray(f["L1_xattn_Wo"].T),
        "fcT": np.ascontiguousarray(f["L0_xattn_fc_w"].T), "expert_b": f["L0_ffn_expert_b"],
        "mask": rows(f["mask_BxS2_ik0"].astype(np.int32)).reshape(P, B, NK),
        "ident": np.eye(P, dtype=np.float32), "zmask": zmask.reshape(P, 256),
        "mask4": (p[:, None] // 32 == np.arange(4)).astype(np.float32),
        "mask8": (p[:, None] // 16 == np.arange(8)).astype(np.float32),
        "iota8": rows(np.arange(E, dtype=np.float32)),
        "g_all": rows(np.concatenate([f["g_xattn"], f["g_ffn"]])),
        "fm_rep": np.ascontiguousarray(np.tile(f["L0_xattn_fm_w"].T, (8, 1))), "fm_b": np.tile(f["L0_xattn_fm_b"], 8).reshape(P, 1),
        "sign": np.where(p % 32 < 16, 1.0, -1.0).astype(np.float32).reshape(P, 1),
        "b1": cols(f["L0_ffn_b1"]), "b2": rows(f["L0_ffn_b2"]), "bq": cols(f["L1_xattn_bq"]),
        "bkv": np.concatenate([cols(f["L1_xattn_bk"]), cols(f["L1_xattn_bv"])], axis=1),
        "rb": rows(f["L1_ffn_router_bias"].reshape(1)),
        "ob": rows(np.concatenate([f["L0_xattn_fc_b"], f["L1_xattn_bo"]])),
    }
    for n in ("L0_ffn_W1", "L0_ffn_W2", "L0_ffn_expert_W", "L1_ffn_router_w", "L1_ffn_gate_w", "L1_ffn_up_w",
              "L1_ffn_down_w", "L1_ffn_s_gate_w", "L1_ffn_s_up_w", "L1_ffn_s_down_w"):
        arrays[n] = f[n]
    nc = bacc.Bacc("TRN2", target_bir_lowering=False, num_devices=1)
    args = {}
    for n, v in arrays.items():
        v = arrays[n] = np.ascontiguousarray(v)
        args[n] = nc.dram_tensor("in_" + n, v.shape, mybir.dt.from_np(v.dtype), kind="ExternalInput").ap()
    args["out"] = nc.dram_tensor("out_x", (B * S, D), F32, kind="ExternalOutput").ap()
    gated_layers(nc, args)
    got = run_bass_kernel_spmd(nc, [{"in_" + n: v for n, v in arrays.items()}], core_ids=[0])
    return got.results[0]["out_x"].reshape(B, S, D)
```

```python
from contextlib import ExitStack

import numpy as np

import concourse.bass as bass
from concourse import mybir

F32 = mybir.dt.float32
F16 = mybir.dt.float16
I32 = mybir.dt.int32
U32 = mybir.dt.uint32
ALU = mybir.AluOpType
ACT = mybir.ActivationFunctionType
AX = mybir.AxisListType.X

P = 128
D = 256
KC = D // P
B = 4
S = 1024
NK = 77
H = 16
TB = 256
SUB = TB // P
NB = B * S // TB
BPB = S // TB
HK = H * NK
GW = HK // 4
NCH = (HK + P - 1) // P
HKP = NCH * P
E = 8
TOPK = 4
NI = 128
NSH = 4
WS = 16.0
EPS = 1e-5
FINITE_LOW = -1.0e30

BANKS = ("T0", "T1", "F0", "F1", "S0", "S1")


LAG = 2
HEAD = 3


def events(step):
    kind, layer, arg = step[0], step[1], step[3:]
    if kind == "aL":
        return {"a_stats": 1, "a_rstd": 1, "a_xn": 1, "a_xb": 1}
    if kind == "aX":
        return {"T0": 1, "a_xh": 1}
    if kind == "aZ":
        return {"T1": 1, "T0": 1} if layer == 0 else {"T1": 1}
    if kind == "aS":
        return {f"S{arg[0] % 2}": 1, "a_exp": 1}
    if kind == "aN":
        return {"a_rs": 1, "a_pn": 1}
    if kind == "aT":
        return {"T1": 2, "T0": 1}
    if kind == "aO":
        return {"T0": 1}
    if kind == "fL":
        return {"f_stats": 1, "f_rstd": 1, "f_xn": 1}
    if kind == "fX":
        return {"T1": 1, "f_xh": 1}
    if kind == "fH":
        return {"T0": 1, "f_hs": 1}
    if kind == "fM":
        return {"T1": 1}
    if kind == "fB":
        return {"T0": 1, "T1": 1}
    if kind == "fE":
        return {f"F{arg[1] % 2}": 1}
    if kind == "fR":
        return {"T0": 1, "f_nmx": 1, "f_re": 1}
    if kind == "fG":
        return {f"F{arg[0] % 2}": 1, "f_th": 1}
    if kind == "fA":
        return {"f_ah": 1, "f_act": 1}
    if kind == "fD":
        return {"T1": 1}
    if kind == "pF":
        return {"T0": 2, "T1": 2}
    if kind == "pW":
        return {"T0": NCH // 2, "T1": NCH // 2, "p_kv": 1}
    if kind == "out":
        return {}
    raise ValueError(kind)


def round_steps(att, ffn, next_att, next_ffn):
    def groups(f):
        if f is None:
            return []
        if f[0] == 0:
            g = [[("fH", *f)], [("fM", *f)]]
            g += [[("fE", *f, s, p)] for p in range(E // 2) for s in range(SUB)]
            g[4] = [("fB", *f, 0), ("fB", *f, 1)] + g[4]
            return g
        g, nj = [], E + NSH
        for j in range(nj + 2):
            g.append([])
            if j < nj:
                g[-1].append(("fG", *f, j))
            if 1 <= j <= nj:
                g[-1].append(("fA", *f, j - 1))
            if 2 <= j < E + 2:
                g[-1].append(("fD", *f, j - 2))
        g[1].append(("fR", *f))
        g[-1] += [("fD", *f, E), ("out", *f)]
        return g

    now, later = groups(ffn)[HEAD:], groups(next_ffn)[:HEAD]
    total = len(now)

    def fill(share):
        n = max(1, round(share * total)) if total else 0
        take, now[:] = now[:n], now[n:]
        return [st for g in take for st in g]

    out = []
    if att is not None:
        out += [("aS", *att, 0), ("aS", *att, 1)] + fill(0.15)
        out += [("aN", *att, 0), ("aS", *att, 2)] + fill(0.15)
        out += [("aN", *att, 1), ("aS", *att, 3)] + fill(0.2)
        out += [("aN", *att, 2)]
    if next_att is not None:
        out += [("aL", *next_att)]
    out += fill(0.15)
    if att is not None:
        out += [("aN", *att, 3)]
    if next_att is not None:
        out += [("aX", *next_att)] + fill(0.1) + [("aZ", *next_att)]
    out += [st for g in now for st in g]
    if next_ffn is not None:
        out += [("fL", *next_ffn)]
    if att is not None:
        out += [("aT", *att, 0), ("aO", *att, 0)]
    if next_ffn is not None:
        out += [("fX", *next_ffn)] + later[0]
    if att is not None:
        out += [("aT", *att, 1)]
    if next_ffn is not None:
        out += later[1]
    if att is not None:
        out += [("aO", *att, 1)]
    return out + [st for g in later[2:] for st in g]


class Tally:

    def __init__(self):
        self.n, self.rate, self.it = {}, {}, None

    def past(self, name, more=0):
        n = self.n.get(name, 0) + more
        if self.it is None:
            return n
        return self.it * self.rate.get(name, 0) + n

    def step(self, names):
        for k, v in names.items():
            self.n[k] = self.n.get(k, 0) + v

    def enter(self, it, rate):
        self.it, self.rate = it, rate

    def leave(self, trips):
        self.it = None
        for k, v in self.rate.items():
            self.n[k] = self.n.get(k, 0) + v * (trips - 1)


class Dry:

    def __getattr__(self, name):
        return lambda *a, **k: self


def gated_layers(nc, a):
    with ExitStack() as ctx:
        def sb(name, shape, dt=F32):
            return ctx.enter_context(nc.sbuf_tensor(name, shape, dt))

        def pb(name, shape):
            return ctx.enter_context(nc.psum_tensor(name, shape, F32))

        x_sb = sb("x_sb", [P, NB * SUB, D])
        ctx_t = sb("ctx_t", [P, KC, B * NK])
        fo_w = sb("fo_w", [P, 4, D])
        k_bd = sb("k_bd", [P, B, HK])
        w_vo = sb("w_vo", [P, B, NCH, D])
        stage = w_vo[:, 2:4, :, :].rearrange("p b c d -> p (b c d)")[:, 0:4096].rearrange(
            "p (a n) -> p a n", a=2)
        probs = sb("probs", [P, SUB, HKP])
        probs_t = sb("probs_t", [P, NCH, P])
        q_t = sb("q_t", [P, 4, TB])
        mv = sb("mv", [P, 2, SUB, 2])
        stats = sb("stats", [P, 2, SUB, 6])
        rstd = sb("rstd", [P, 2, SUB])
        xn = sb("xn", [P, 2, SUB, D])
        kv_w = xn
        xh = sb("xh", [P, 2, KC, TB], F16)
        xl = sb("xl", [P, 2, KC, TB], F16)
        row_max = sb("row_max", [P, 2, 8])
        row_inv = sb("row_inv", [P, 2, 2, 8])
        h_hi = sb("h_hi", [P, TB], F16)
        h_lo = sb("h_lo", [P, TB], F16)
        one_hot = sb("one_hot", [P, SUB, P], F16)
        one_hot_t = sb("one_hot_t", [P, P], F16)
        gate = sb("gate", [P, SUB, E])
        logits, top, shifted, expo, score, corrected, rank, chosen, kept = (
            sb(n, [P, SUB, E]) for n in ("logits", "top", "shifted", "expo", "score", "corrected", "rank",
                                         "chosen", "kept"))
        match = sb("match", [P, SUB, E, TOPK])
        total = sb("total", [P, 4, SUB])
        unused = sb("unused", [P, 1])
        idx = sb("idx", [P, SUB, 8], U32)
        th = sb("th", [P, 2, TB])
        h_t = th[:, 0, :]
        act_f = sb("act_f", [P, 2, TB])
        act = sb("act", [P, 2, E + NSH, TB], F16)
        padded = act[:, :, :, :].rearrange("p a j t -> p (a j t)").bitcast(F32)
        feat = probs[:, :, :].rearrange("p s c -> p (s c)")[:, 0:4 * B * NK].rearrange(
            "p (g c) -> p g c", g=4)
        zw32 = sb("zw32", [P, 2, P])
        msk = sb("msk", [P, B, NK])
        mask_i = msk[:, :, :].bitcast(I32)
        x_bias = sb("x_bias", [P, 2, D])
        tg = sb("tg", [P, 4])
        tgw = sb("tgw", [P, 2])
        eps_t = sb("eps_t", [P, SUB])
        rs_exp = sb("rs_exp", [P, SUB])

        consts = {}
        consts["zmask"] = xn[:, 0, 0, :]
        consts["ob"] = q_t[:, 0:2, :].rearrange("p a n -> p (a n)")
        for name, shape in CONSTS.items():
            if name in consts:
                continue
            consts[name] = sb("c_" + name, [P] + list(shape))
        ident, zmask, mask4, mask8, iota8 = (consts[n] for n in ("ident", "zmask", "mask4", "mask8", "iota8"))
        ident16 = sb("ident16", [P, P], F16)

        def split(name, shape):
            return sb(name + "_h", [P] + shape, F16), sb(name + "_l", [P] + shape, F16)

        zw = split("zw", [2, P])
        w1 = split("w1", [KC, P])
        w2 = split("w2", [E])
        ew = split("ew", [KC, E, D])
        eb = split("eb", [D])
        wq = split("wq", [KC, D])
        rw = split("rw", [KC, E])
        gw = split("gw", [KC, E + NSH, NI])
        uw = split("uw", [KC, E + NSH, NI])
        dw = split("dw", [E + NSH, D])

        bank = {n: pb("ps_" + n, [P, 512]) for n in ("T0", "T1", "F0", "F1")}
        bank["S0"] = pb("ps_S0", [P, 2, 512])
        bank["S1"] = pb("ps_S1", [P, 2, 512])

        def sem(name):
            return ctx.enter_context(nc.semaphore(name))

        filled = {n: sem("filled_" + n) for n in BANKS}
        read = {n: sem("read_" + n) for n in BANKS}
        ev = {n: sem(n) for n in (
            "a_stats", "a_rstd", "a_xn", "a_xb", "a_xh", "a_exp", "a_rs", "a_pn",
            "f_stats", "f_rstd", "f_xn", "f_xh", "f_hs", "f_nmx", "f_re",
            "f_th", "f_ah", "f_act", "p_kv")}
        small_in = sem("small_in")
        x_in = sem("x_in")
        stage_in = [sem("stage_in0"), sem("stage_in1")]
        split_hi = sem("split_hi")
        split_lo = sem("split_lo")
        ready = sem("ready")
        tanh_done = sem("tanh_done")
        fo_in = sem("fo_in")
        out_done = sem("out_done")
        dve_seq = sem("dve_seq")
        pool_seq = sem("pool_seq")

        def part(src, pair, sl):
            return src, sl(pair[0]), sl(pair[1])

        def kcn(w):
            return w.rearrange("(c p) n -> p c n", p=P)

        pieces = [part(kcn(a["L0_ffn_W1"]), w1, lambda t: t[:, :, :]),
                  part(a["L0_ffn_W2"], w2, lambda t: t[:, :])]
        for c in range(KC):
            src = a["L0_ffn_expert_W"].rearrange("e (c p) n -> c p e n", p=P)[c]
            pieces.append(part(src, ew, lambda t, c=c: t[:, c, :, :]))
        pieces += [part(a["expert_b"], eb, lambda t: t[:, :]),
                   part(kcn(a["WqT"]), wq, lambda t: t[:, :, :]),
                   part(kcn(a["L1_ffn_router_w"]), rw, lambda t: t[:, :, :])]
        for nm, sh, w in (("gate_w", "s_gate_w", gw), ("up_w", "s_up_w", uw)):
            for c in range(KC):
                src = a["L1_ffn_" + nm].rearrange("e (c p) n -> c p e n", p=P)[c]
                pieces.append(part(src, w, lambda t, c=c: t[:, c, 0:E, :]))
                src = a["L1_ffn_" + sh].rearrange("(c p) (j n) -> c p j n", p=P, n=NI)[c]
                pieces.append(part(src, w, lambda t, c=c: t[:, c, E:E + NSH, :]))
        pieces.append(part(a["L1_ffn_down_w"].rearrange("e p n -> p e n"), dw, lambda t: t[:, 0:E, :]))
        pieces.append(part(a["L1_ffn_s_down_w"].rearrange("(j p) n -> p j n", p=P), dw,
                           lambda t: t[:, E:E + NSH, :]))

        def staged(k, like):
            n = int(np.prod(like.shape[1:]))
            v = stage[:, k % 2, 0:n]
            if len(like.shape) == 3:
                v = v.rearrange("p (a b) -> p a b", b=like.shape[2])
            return v

        small_loads = [(ctx_t, a["ctxT"].rearrange("(c p) n -> p c n", p=P)),
                       (mask_i, a["mask"])]
        small_loads += [(consts[n], a[n]) for n in CONSTS]

        def prog(walk):
            def steps(k):
                def rel(j):
                    return (j // NB, j % NB - k % NB) if 0 <= j < 2 * NB else None
                return round_steps(rel(k), rel(k - LAG), rel(k + 1), rel(k + 1 - LAG))

            def pre(layer):
                return [("pF", layer, 0)] + [("pW", layer, 0, b) for b in range(B)]

            walk(pre(0) + [("aL", 0, 0), ("aX", 0, 0), ("aZ", 0, 0)], 0)
            for layer in range(2):
                k0 = layer * NB
                if layer == 1:
                    walk(pre(1), 0)
                for k in range(LAG):
                    walk(steps(k0 + k), k)
                walk(steps(k0 + LAG), LAG, trips=NB - 1 - LAG)
                walk(steps(k0 + NB - 1), NB - 1)
            for k in range(2 * NB, 2 * NB + LAG):
                walk(steps(k), k % NB)

        def run(eng, handle):
            t = Tally()

            def walk(steps, rnd, trips=None):
                def body(e, i):
                    for st in steps:
                        handle(e, t, st, rnd + st[2] if i is None else i + (rnd + st[2]))
                        t.step(events(st))

                if trips is None:
                    body(eng, None)
                    return
                before = dict(t.n)
                body(Dry(), 0)
                rate = {k: v - before.get(k, 0) for k, v in t.n.items()}
                t.n = before
                with eng.Fori(0, trips) as i:
                    t.enter(i, rate)
                    body(eng, i)
                t.leave(trips)

            prog(walk)

        def at_least(e, s, n):
            if not (isinstance(n, int) and n <= 0):
                e.wait_ge(s, n)

        block = ctx.enter_context(nc.Block())

        @block.sync
        def _(sp):
            for dst, src in small_loads:
                sp.dma_start(dst[tuple([slice(None)] * len(dst.shape))], src).then_inc(small_in, 16)
            sp.dma_start(fo_w[:, :, :], a["fcT"].rearrange("(g p) n -> p g n", p=P)).then_inc(small_in, 16)
            for b in range(B):
                sp.dma_start(x_sb[:, b * 8:(b + 1) * 8, :],
                             a["x"][b].rearrange("(t p) d -> p t d", p=P)).then_inc(x_in, 16)
            for k, (src, hi, _) in enumerate(pieces):
                if k >= 2:
                    sp.wait_ge(split_lo, k - 1)
                np_ = src.shape[0]
                sp.dma_start(staged(k, hi)[0:np_], src).then_inc(stage_in[k % 2], 16)

            def handle(e, t, st, blk):
                if st[0] == "out":
                    e.wait_ge(read["T1"], t.past("T1"))
                    dst = a["out"].rearrange("(t p) d -> p t d", p=P)
                    e.dma_start(dst[:, bass.ts(blk, SUB), :],
                                x_sb[:, bass.ts(blk, SUB), :]).then_inc(out_done, 16)
                if st[0] == "pF" and st[1] == 1:
                    at_least(e, read["T0"], t.past("T0"))
                    e.wait_ge(ev["a_xh"], t.past("a_xh"))
                    e.wait_ge(ev["f_xh"], t.past("f_xh"))
                    at_least(e, read["T1"], t.past("T1"))
                    e.dma_start(kv_w[:, 0], kcn(a["WkT"])).then_inc(fo_in, 16)
                    e.dma_start(kv_w[:, 1], kcn(a["WvT"])).then_inc(fo_in, 16)
                    e.dma_start(fo_w[:, 0:KC, :], kcn(a["WoT"])).then_inc(fo_in, 16)

            run(sp, handle)
            sp.wait_ge(out_done, 16 * NB)

        @block.tensor
        def _(pe):
            def mm3(e, out, lh, ll, rh, rl, first, last):
                e.matmul(out, lh, rh, start=first, stop=False)
                e.matmul(out, lh, rl, start=False, stop=False)
                return e.matmul(out, ll, rh, start=False, stop=last)

            pe.wait_ge(ready, 1)

            def handle(e, t, st, blk):
                kind, layer = st[0], st[1]

                def take(name, use=0):
                    at_least(e, read[name], t.past(name, use))

                if kind == "pF":
                    if layer == 1:
                        e.wait_ge(fo_in, 48)
                    for g in range(4):
                        bk = f"T{g % 2}"
                        take(bk, g // 2)
                        o = bank[bk][:, 0:B * NK]
                        if layer == 0:
                            mm = e.matmul(o, zw32[:, g % 2, :], ctx_t[:, g // 2, :], start=True, stop=True)
                        else:
                            for c in range(KC):
                                mm = e.matmul(o, kv_w[:, g // 2, c, (g % 2) * P:(g % 2) * P + P],
                                              ctx_t[:, c, :], start=(c == 0), stop=(c == KC - 1))
                        mm.then_inc(filled[bk], 1)
                if kind == "pW":
                    e.wait_ge(ev["p_kv"], t.past("p_kv", 1))
                    gw_, ng = (GW, 4) if layer == 0 else (2 * GW, 2)
                    pv = padded[:, 0:ng * (gw_ + 2 * P)].rearrange("p (g c) -> p g c", g=ng)
                    for c in range(NCH):
                        bk = f"T{c % 2}"
                        take(bk, c // 2)
                        gs = [g for g in range(ng) if P * c < gw_ * (g + 1) and P * (c + 1) > gw_ * g]
                        for g in gs:
                            at = P + P * c - gw_ * g
                            mm = e.matmul(bank[bk][:, 0:D], pv[:, g, at:at + P], fo_w[:, g, :],
                                          start=(g == gs[0]), stop=(g == gs[-1]))
                        mm.then_inc(filled[bk], 1)
                if kind in ("aX", "fX"):
                    w = 0 if kind == "aX" else 1
                    bk = "T0" if w == 0 else "T1"
                    e.wait_ge(ev["a_xn" if w == 0 else "f_xn"], t.past("a_xn" if w == 0 else "f_xn"))
                    take(bk)
                    for c in range(KC):
                        for s in range(SUB):
                            mm = e.transpose(bank[bk][:, c * TB + s * P:c * TB + s * P + P],
                                             xn[:, w, s, c * P:c * P + P], ident[:, :])
                    mm.then_inc(filled[bk], 1)
                if kind == "aZ":
                    e.wait_ge(read["T0"], t.past("T0"))
                    for o4 in range(4 if layer == 0 else KC):
                        bk = f"T{1 - o4 // 2}"
                        if o4 % 2 == 0:
                            take(bk)
                        o = bank[bk][:, (o4 % 2) * TB:(o4 % 2) * TB + TB]
                        if layer == 0:
                            mm = mm3(e, o, zw[0][:, o4 % 2, :], zw[1][:, o4 % 2, :],
                                     xh[:, 0, o4 // 2, :], xl[:, 0, o4 // 2, :], True, True)
                        else:
                            for c in range(KC):
                                cols = slice(o4 * P, o4 * P + P)
                                mm = mm3(e, o, wq[0][:, c, cols], wq[1][:, c, cols], xh[:, 0, c, :],
                                         xl[:, 0, c, :], c == 0, c == KC - 1)
                        if o4 % 2 == 1:
                            mm.then_inc(filled[bk], 1)
                if kind == "aS":
                    u = st[3]
                    s, half = u // 2, u % 2
                    bk = f"S{u % 2}"
                    if u == 0:
                        e.wait_ge(read["T1"], t.past("T1"))
                        e.wait_ge(read["T0"], t.past("T0"))
                    take(bk)
                    for gg in range(2):
                        q = (2 * half + gg) if layer == 0 else half
                        at = (2 * half + gg) * GW
                        mm = e.matmul(bank[bk][:, gg, 0:GW], q_t[:, q, s * P:s * P + P],
                                      k_bd[:, blk // BPB, at:at + GW], start=True, stop=True)
                    mm.then_inc(filled[bk], 1)
                if kind == "aT":
                    s = st[3]
                    e.wait_ge(ev["a_pn"], t.past("a_pn"))
                    for piece, bk in enumerate(("T1", "T0", "T1")):
                        take(bk, 1 if piece == 2 else 0)
                        for c in range(4 * piece, min(4 * piece + 4, NCH)):
                            mm = e.transpose(bank[bk][:, (c % 4) * P:(c % 4) * P + P],
                                             probs[:, s, c * P:c * P + P], ident[:, :])
                        mm.then_inc(filled[bk], 1)
                if kind == "aO":
                    e.wait_ge(read["T0"], t.past("T0"))
                    e.wait_ge(read["T1"], t.past("T1"))
                    for c in range(NCH):
                        mm = e.matmul(bank["T0"][:, 0:D], probs_t[:, c, :], w_vo[:, blk // BPB, c, :],
                                      start=(c == 0), stop=(c == NCH - 1))
                    mm.then_inc(filled["T0"], 1)
                if kind == "fH":
                    e.wait_ge(read["T1"], t.past("T1"))
                    take("T0")
                    for c in range(KC):
                        mm = mm3(e, bank["T0"][:, 0:TB], w1[0][:, c, :], w1[1][:, c, :],
                                 xh[:, 1, c, :], xl[:, 1, c, :], c == 0, c == KC - 1)
                    mm.then_inc(filled["T0"], 1)
                if kind == "fM":
                    e.wait_ge(ev["f_hs"], t.past("f_hs"))
                    take("T1")
                    for s in range(SUB):
                        tok = slice(s * P, s * P + P)
                        mm = mm3(e, bank["T1"][:, s * E:s * E + E], h_hi[:, tok], h_lo[:, tok],
                                 w2[0][:, :], w2[1][:, :], True, True)
                    mm.then_inc(filled["T1"], 1)
                if kind == "fB":
                    s = st[3]
                    e.wait_ge(read["T1"], t.past("T1"))
                    take("T0")
                    e.transpose(bank["T0"][:, 0:P // 2].bitcast(F16), one_hot[:, s, :],
                                ident16[:, :]).then_inc(filled["T0"], 1)
                    e.wait_ge(read["T0"], t.past("T0", 1))
                    take("T1")
                    e.matmul(bank["T1"][:, 0:D], one_hot_t[:, :], eb[0][:, :], start=True, stop=False)
                    e.matmul(bank["T1"][:, 0:D], one_hot_t[:, :], eb[1][:, :], start=False,
                             stop=True).then_inc(filled["T1"], 1)
                if kind == "fE":
                    s, p2 = st[3], st[4]
                    bk = f"F{p2 % 2}"
                    take(bk)
                    tok = slice(s * P, s * P + P)
                    for c in range(KC):
                        mm = mm3(e, bank[bk][:, :], xh[:, 1, c, tok], xl[:, 1, c, tok],
                                 ew[0][:, c, 2 * p2:2 * p2 + 2, :], ew[1][:, c, 2 * p2:2 * p2 + 2, :],
                                 c == 0, c == KC - 1)
                    mm.then_inc(filled[bk], 1)
                if kind == "fR":
                    take("T0")
                    for s in range(SUB):
                        tok = slice(s * P, s * P + P)
                        for c in range(KC):
                            mm = mm3(e, bank["T0"][:, s * E:s * E + E], xh[:, 1, c, tok], xl[:, 1, c, tok],
                                     rw[0][:, c, :], rw[1][:, c, :], c == 0, c == KC - 1)
                    mm.then_inc(filled["T0"], 1)
                if kind == "fG":
                    j = st[3]
                    bk = f"F{j % 2}"
                    if j == 0:
                        e.wait_ge(read["T1"], t.past("T1"))
                    take(bk)
                    for m, w in enumerate((gw, uw)):
                        for c in range(KC):
                            mm = mm3(e, bank[bk][:, m * TB:m * TB + TB], w[0][:, c, j, :],
                                     w[1][:, c, j, :], xh[:, 1, c, :], xl[:, 1, c, :],
                                     c == 0, c == KC - 1)
                    mm.then_inc(filled[bk], 1)
                if kind == "fD":
                    j = st[3]
                    js = [j] if j < E else list(range(E, E + NSH))
                    e.wait_ge(ev["f_act"], t.past("f_act", -1 if j < E else 0))
                    take("T1")
                    for s in range(SUB):
                        tok = slice(s * P, s * P + P)
                        for jj in js:
                            mm = mm3(e, bank["T1"][:, s * D:s * D + D], act[:, 0, jj, tok],
                                     act[:, 1, jj, tok], dw[0][:, jj, :], dw[1][:, jj, :],
                                     jj == js[0], jj == js[-1])
                    mm.then_inc(filled["T1"], 1)

            run(pe, handle)

        @block.scalar
        def _(sc):
            sc.wait_ge(small_in, 16 * (len(small_loads) + 1))
            sc.activation(tg[:, :], consts["g_all"][:, :], ACT.Tanh).then_inc(tanh_done, 1)
            for k, (src, hi, _) in enumerate(pieces):
                sc.wait_ge(stage_in[k % 2], 16 * (k // 2 + 1))
                np_ = src.shape[0]
                sc.activation(hi[0:np_], staged(k, hi)[0:np_], ACT.Copy, scale=WS).then_inc(split_hi, 1)

            def handle(e, t, st, blk):
                kind, layer = st[0], st[1]

                def got(name, use=0):
                    e.wait_ge(filled[name], t.past(name, use + 1))

                if kind == "pF":
                    if layer == 0:
                        e.wait_ge(ready, 1)
                    for g in range(4):
                        bk = f"T{g % 2}"
                        got(bk, g // 2)
                        if layer == 0:
                            e.activation(feat[:, g, :], bank[bk][:, 0:B * NK], ACT.Exp,
                                         bias=consts["fm_b"][:, 0:1]).then_inc(read[bk], 1)
                        else:
                            bias = consts["bkv"][:, g:g + 1]
                            e.activation(feat[:, g, :], bank[bk][:, 0:B * NK], ACT.Identity,
                                         bias=bias).then_inc(read[bk], 1)
                if kind == "pW":
                    for c in range(NCH):
                        bk = f"T{c % 2}"
                        got(bk, c // 2)
                        e.activation(w_vo[:, st[3], c, :], bank[bk][:, 0:D], ACT.Copy,
                                     scale=tg[:, layer:layer + 1]).then_inc(read[bk], 1)
                if kind in ("aX", "fX"):
                    w = 0 if kind == "aX" else 1
                    bk = "T0" if w == 0 else "T1"
                    got(bk)
                    e.activation(xh[:, w, :, :], bank[bk][:, :].rearrange("p (c t) -> p c t", c=KC),
                                 ACT.Copy).then_inc(ev["a_xh" if w == 0 else "f_xh"], 1)
                if kind == "aZ":
                    for o2 in range(2 if layer == 0 else 1):
                        bk = f"T{1 - o2}"
                        got(bk)
                        z = bank[bk][:, :].rearrange("p (c t) -> p c t", c=2)
                        if layer == 0:
                            e.activation(q_t[:, 2 * o2:2 * o2 + 2, :], z, ACT.Exp, scale=1.0 / WS,
                                         bias=consts["fm_b"][:, 0:1]).then_inc(read[bk], 1)
                        else:
                            e.activation(q_t[:, 0, :], z[:, 0, :], ACT.Identity, scale=1.0 / WS,
                                         bias=consts["bq"][:, 0:1])
                            e.activation(q_t[:, 1, :], z[:, 1, :], ACT.Identity, scale=1.0 / WS,
                                         bias=consts["bq"][:, 1:2]).then_inc(read[bk], 1)
                if kind == "aS":
                    u = st[3]
                    s, half = u // 2, u % 2
                    bk = f"S{u % 2}"
                    e.wait_ge(read[bk], t.past(bk, 1))
                    v = probs[:, s, half * 2 * GW:(half + 1) * 2 * GW]
                    scale = 1.0 / 16.0 if layer == 0 else 0.25
                    e.activation(v, v, ACT.Exp, scale=scale).then_inc(ev["a_exp"], 1)
                if kind == "aT":
                    for piece, bk in enumerate(("T1", "T0", "T1")):
                        got(bk, 1 if piece == 2 else 0)
                        n = min(4, NCH - 4 * piece)
                        e.activation(probs_t[:, 4 * piece:4 * piece + n, :],
                                     bank[bk][:, 0:n * P].rearrange("p (c t) -> p c t", c=n),
                                     ACT.Copy).then_inc(read[bk], 1)
                if kind == "fH":
                    got("T0")
                    e.activation(h_t, bank["T0"][:, 0:TB], ACT.Relu, scale=1.0 / WS,
                                 bias=consts["b1"][:, 0:1]).then_inc(read["T0"], 1)
                if kind == "fB":
                    got("T0")
                    e.activation(one_hot_t[:, :], bank["T0"][:, 0:P // 2].bitcast(F16),
                                 ACT.Copy).then_inc(read["T0"], 1)
                if kind == "fR":
                    e.wait_ge(ev["f_nmx"], t.past("f_nmx", 1))
                    e.activation(expo[:, :, :], shifted[:, :, :], ACT.Exp).then_inc(ev["f_re"], 1)
                if kind == "fG":
                    j = st[3]
                    got(f"F{j % 2}")
                    e.activation(th[:, j % 2, :], bank[f"F{j % 2}"][:, 0:TB], ACT.Tanh,
                                 scale=0.5 / WS).then_inc(ev["f_th"], 1)
                if kind == "fA":
                    j = st[3]
                    bk = f"F{j % 2}"
                    e.wait_ge(read[bk], t.past(bk))
                    e.activation(act[:, 0, j, :], act_f[:, j % 2, :], ACT.Copy).then_inc(ev["f_ah"], 1)

            run(sc, handle)

        @block.gpsimd
        def _(pool):
            pool.memset(one_hot[:, :, :], 0.0)
            pool.memset(eb[0][:, :], 0.0)
            pool.memset(eb[1][:, :], 0.0)
            pool.memset(eps_t[:, :], EPS)
            pool.memset(rs_exp[:, :], -0.5).then_inc(pool_seq, 1)
            pool.wait_ge(pool_seq, 1)

            def handle(e, t, st, blk):
                kind, layer = st[0], st[1]

                def link(ins):
                    ins.then_inc(pool_seq, 1)
                    e.wait_ge(pool_seq, t.past("pool_seq", 2))
                    t.step({"pool_seq": 1})

                if kind in ("aL", "fL"):
                    w = 0 if kind == "aL" else 1
                    pre = "a" if w == 0 else "f"
                    e.wait_ge(ev[pre + "_stats"], t.past(pre + "_stats", 1))
                    link(e.tensor_tensor(rstd[:, w, :], mv[:, w, :, 1], eps_t[:, :], ALU.add))
                    e.tensor_tensor(rstd[:, w, :], rstd[:, w, :], rs_exp[:, :],
                                    ALU.pow).then_inc(ev[pre + "_rstd"], 1)
                    if w == 0:
                        e.wait_ge(ev["a_xn"], t.past("a_xn", 1))
                        xs = x_sb[:, bass.ts(blk, SUB), :]
                        e.tensor_tensor(xs, xs, x_bias[:, layer, :].unsqueeze(1).broadcast_to([P, SUB, D]),
                                        ALU.add).then_inc(ev["a_xb"], 1)
                if kind == "fA":
                    j = st[3]
                    e.wait_ge(ev["f_ah"], t.past("f_ah", 1))
                    e.tensor_tensor(act[:, 1, j, :], act_f[:, j % 2, :], act[:, 0, j, :],
                                    ALU.subtract).then_inc(ev["f_act"], 1)
                if kind == "aN":
                    u = st[3]
                    s, half = u // 2, u % 2
                    e.wait_ge(ev["a_rs"], t.past("a_rs", 1))
                    v = probs[:, s, half * 2 * GW:(half + 1) * 2 * GW].rearrange("p (h k) -> p h k", k=NK)
                    e.tensor_tensor(v, v, row_inv[:, 1, u % 2, :].unsqueeze(2).broadcast_to([P, 8, NK]),
                                    ALU.mult).then_inc(ev["a_pn"], 1)

            run(pool, handle)

        @block.vector
        def _(dve):
            start = Tally()

            def chain(e, t, ins):
                ins.then_inc(dve_seq, 1)
                e.wait_ge(dve_seq, t.past("dve_seq", 1))
                t.step({"dve_seq": 1})

            dve.wait_ge(small_in, 16 * (len(small_loads) + 1))
            dve.wait_ge(tanh_done, 1)
            dve.wait_ge(pool_seq, 1)
            chain(dve, start, dve.tensor_tensor(
                zw32[:, :, :].rearrange("p a (g e) -> p (a g) e", e=16),
                consts["fm_rep"][:, :].unsqueeze(1).broadcast_to([P, 16, 16]),
                zmask[:, :].rearrange("p (g e) -> p g e", e=16), ALU.mult))
            chain(dve, start, dve.tensor_scalar(zw[0][:, :, :], zw32[:, :, :], WS, None, ALU.mult))
            chain(dve, start, dve.scalar_tensor_tensor(zw[1][:, :, :], zw32[:, :, :], WS, zw[0][:, :, :],
                                                       ALU.mult, ALU.subtract))
            dve.tensor_copy(ident16[:, :], ident[:, :])
            chain(dve, start, dve.tensor_tensor(consts["fm_b"][:, :], consts["fm_b"][:, :],
                                                consts["sign"][:, :], ALU.mult))
            dve.memset(padded[:, :], 0.0)
            chain(dve, start, dve.tensor_scalar(msk[:, :, :], mask_i[:, :, :], 0.0, FINITE_LOW,
                                                ALU.is_equal, ALU.mult))
            dve.tensor_scalar(tgw[:, :], tg[:, 2:4], 1.0 / WS, None, ALU.mult)
            for layer in range(2):
                dve.tensor_scalar(x_bias[:, layer, :], consts["ob"][:, layer * D:layer * D + D],
                                  tg[:, layer:layer + 1], None, ALU.mult)
            chain(dve, start, dve.memset(probs[:, :, HK:HKP], 0.0))
            for k, (src, hi, lo) in enumerate(pieces):
                dve.wait_ge(split_hi, k + 1)
                np_ = src.shape[0]
                dve.scalar_tensor_tensor(lo[0:np_], staged(k, hi)[0:np_], WS, hi[0:np_], ALU.mult,
                                         ALU.subtract).then_inc(split_lo, 1)
            dve.wait_ge(x_in, 16 * B)
            dve.wait_ge(split_lo, len(pieces))
            dve.tensor_copy(unused[:, :], iota8[:, 0:1]).then_inc(ready, 1)
            base = start.n["dve_seq"]

            def handle(e, t, st, blk):
                kind, layer = st[0], st[1]

                def link(ins):
                    ins.then_inc(dve_seq, 1)
                    e.wait_ge(dve_seq, t.past("dve_seq", base + 1))
                    t.step({"dve_seq": 1})

                def settle(e):
                    e.tensor_copy(unused[:, :], iota8[:, 0:1])

                def got(name, use=0):
                    e.wait_ge(filled[name], t.past(name, use + 1))

                def mine(name, use=0):
                    e.wait_ge(read[name], t.past(name, use + 1))

                if kind == "pW":
                    b = st[3]
                    ng, nh, mk = (4, 4, mask4) if layer == 0 else (2, 8, mask8)
                    gw_ = nh * NK
                    if b == 0:
                        e.wait_ge(read["T0"], t.past("T0"))
                        e.wait_ge(read["T1"], t.past("T1"))
                        if layer == 1:
                            link(e.memset(padded[:, 0:ng * (gw_ + 2 * P)], 0.0))
                    else:
                        e.wait_ge(filled["T1"], t.past("T1"))
                        e.wait_ge(filled["T0"], t.past("T0"))
                    pv = padded[:, 0:ng * (gw_ + 2 * P)].rearrange("p (g c) -> p g c", g=ng)
                    for g in range(ng):
                        head = mk[:, :].unsqueeze(2).broadcast_to([P, nh, NK])
                        kf = feat[:, g, b * NK:b * NK + NK].unsqueeze(1).broadcast_to([P, nh, NK])
                        vf = kf if layer == 0 else feat[:, 2 + g, b * NK:b * NK + NK].unsqueeze(1).broadcast_to(
                            [P, nh, NK])
                        e.tensor_tensor(k_bd[:, b, g * gw_:(g + 1) * gw_].rearrange("p (h k) -> p h k", k=NK),
                                        kf, head, ALU.mult)
                        last = e.tensor_tensor(pv[:, g, P:P + gw_].rearrange("p (h k) -> p h k", k=NK),
                                               vf, head, ALU.mult)
                    last.then_inc(ev["p_kv"], 1)
                if kind in ("aL", "fL"):
                    w = 0 if kind == "aL" else 1
                    pre = "a" if w == 0 else "f"
                    if w == 1:
                        at_least(e, read["T0"], t.past("T0"))
                    for s in range(SUB):
                        ins = e.bn_stats(stats[:, w, s, :], x_sb[:, blk * SUB + s, :])
                    link(ins)
                    settle(e)
                    for s in range(SUB):
                        ins = e.bn_aggr(mv[:, w, s, :], stats[:, w, s, :])
                    ins.then_inc(ev[pre + "_stats"], 1)
                    at_least(e, ev[pre + "_xh"], t.past(pre + "_xh"))
                    e.wait_ge(ev[pre + "_rstd"], t.past(pre + "_rstd", 1))
                    for s in range(SUB):
                        ins = e.tensor_scalar(xn[:, w, s, :], x_sb[:, blk * SUB + s, :], mv[:, w, s, 0:1],
                                              rstd[:, w, s:s + 1], ALU.subtract, ALU.mult)
                    ins.then_inc(ev[pre + "_xn"], 1)
                if kind in ("aX", "fX"):
                    w = 0 if kind == "aX" else 1
                    bk, evn = ("T0", "a_xh") if w == 0 else ("T1", "f_xh")
                    e.wait_ge(ev[evn], t.past(evn, 1))
                    e.tensor_tensor(xl[:, w, :, :], bank[bk][:, :].rearrange("p (c t) -> p c t", c=KC),
                                    xh[:, w, :, :], ALU.subtract).then_inc(read[bk], 1)
                if kind == "aS":
                    u = st[3]
                    s, half = u // 2, u % 2
                    bk = f"S{u % 2}"
                    got(bk)
                    sc_ = bank[bk][:, :, 0:GW].rearrange("p g (h k) -> p g h k", k=NK)
                    v = probs[:, s, half * 2 * GW:(half + 1) * 2 * GW]
                    v4 = v.rearrange("p (g h k) -> p g h k", g=2, k=NK)
                    m = row_max[:, u % 2, :]
                    if layer == 1:
                        mk = msk[:, blk // BPB, :].unsqueeze(1).unsqueeze(1).broadcast_to([P, 2, 4, NK])
                        link(e.tensor_tensor(v4, sc_, mk, ALU.add))
                        sc_ = v4
                    link(e.tensor_reduce(m.rearrange("p (g h) -> p g h", g=2), sc_, AX, ALU.max))
                    mb = m.rearrange("p (g h) -> p g h", g=2).unsqueeze(3).broadcast_to([P, 2, 4, NK])
                    e.tensor_tensor(v4, sc_, mb, ALU.subtract).then_inc(read[bk], 1)
                if kind == "aN":
                    u = st[3]
                    s, half = u // 2, u % 2
                    e.wait_ge(ev["a_exp"], t.past("a_rs", 1))
                    v = probs[:, s, half * 2 * GW:(half + 1) * 2 * GW].rearrange("p (h k) -> p h k", k=NK)
                    if u >= 2:
                        e.wait_ge(ev["a_pn"], t.past("a_pn", -1))
                    link(e.tensor_reduce(row_inv[:, 0, u % 2, :], v, AX, ALU.add))
                    e.reciprocal(row_inv[:, 1, u % 2, :], row_inv[:, 0, u % 2, :]).then_inc(ev["a_rs"], 1)
                if kind == "aO":
                    s = st[3]
                    got("T0")
                    e.wait_ge(ev["a_xb"], t.past("a_xb"))
                    xs = x_sb[:, blk * SUB + s, :]
                    e.tensor_tensor(xs, bank["T0"][:, 0:D], xs, ALU.add).then_inc(read["T0"], 1)
                if kind == "fH":
                    e.wait_ge(read["T0"], t.past("T0", 1))
                    link(e.tensor_copy(h_hi[:, :], h_t))
                    e.tensor_tensor(h_lo[:, :], h_t, h_hi[:, :], ALU.subtract).then_inc(ev["f_hs"], 1)
                if kind == "fM":
                    got("T1")
                    link(e.scalar_tensor_tensor(
                        logits[:, :, :], bank["T1"][:, 0:SUB * E].rearrange("p (s e) -> p s e", e=E), 1.0 / WS,
                        consts["b2"][:, :].unsqueeze(1).broadcast_to([P, SUB, E]), ALU.mult, ALU.add))
                    settle(e)
                    for s in range(SUB):
                        ins = e.max(top[:, s, :], logits[:, s, :])
                    link(ins)
                    settle(e)
                    for s in range(SUB):
                        ins = e.max_index(idx[:, s, :], top[:, s, :], logits[:, s, :])
                    link(ins)
                    link(e.tensor_copy(rank[:, :, :], idx[:, :, :]))
                    for s in range(SUB):
                        e.tensor_scalar(gate[:, s, :], iota8[:, :], rank[:, s, 0:1], tgw[:, 0:1],
                                        ALU.is_equal, ALU.mult)
                        e.tensor_scalar(one_hot[:, s, 0:E], iota8[:, :], rank[:, s, 0:1], None, ALU.is_equal)
                    e.tensor_copy(unused[:, :], iota8[:, 0:1]).then_inc(read["T1"], 1)
                if kind == "fB":
                    s = st[3]
                    got("T1")
                    xs = x_sb[:, blk * SUB + s, :]
                    e.wait_ge(read["F0"], t.past("F0"))
                    e.scalar_tensor_tensor(xs, bank["T1"][:, 0:D], tgw[:, 0:1], xs, ALU.mult,
                                           ALU.add).then_inc(read["T1"], 1)
                    mine("T1")
                if kind == "fE":
                    s, p2 = st[3], st[4]
                    bk = f"F{p2 % 2}"
                    got(bk)
                    xs = x_sb[:, blk * SUB + s, :]
                    link(e.scalar_tensor_tensor(xs, bank[bk][:, 0:D], gate[:, s, 2 * p2:2 * p2 + 1], xs,
                                                ALU.mult, ALU.add))
                    e.scalar_tensor_tensor(xs, bank[bk][:, D:2 * D], gate[:, s, 2 * p2 + 1:2 * p2 + 2], xs,
                                           ALU.mult, ALU.add).then_inc(read[bk], 1)
                    mine(bk)
                if kind == "fR":
                    def wide(col):
                        return col.broadcast_to([P, SUB, E])

                    got("T0")
                    e.tensor_scalar(logits[:, :, :], bank["T0"][:, 0:SUB * E].rearrange("p (s e) -> p s e", e=E),
                                    1.0 / WS, None, ALU.mult).then_inc(read["T0"], 1)
                    mine("T0")
                    settle(e)
                    for s in range(SUB):
                        ins = e.max(top[:, s, :], logits[:, s, :])
                    link(ins)
                    e.tensor_tensor(shifted[:, :, :], logits[:, :, :], wide(top[:, :, 0:1]),
                                    ALU.subtract).then_inc(ev["f_nmx"], 1)
                    e.wait_ge(ev["f_re"], t.past("f_re", 1))
                    link(e.tensor_reduce(total[:, 0, :], expo[:, :, :], AX, ALU.add))
                    link(e.reciprocal(total[:, 1, :], total[:, 0, :]))
                    link(e.tensor_tensor(score[:, :, :], expo[:, :, :], wide(total[:, 1, :].unsqueeze(2)),
                                         ALU.mult))
                    link(e.tensor_scalar(corrected[:, :, :], score[:, :, :], consts["rb"][:, 0:1], None,
                                         ALU.add))
                    settle(e)
                    for s in range(SUB):
                        ins = e.max(top[:, s, :], corrected[:, s, :])
                    link(ins)
                    settle(e)
                    for s in range(SUB):
                        ins = e.max_index(idx[:, s, :], top[:, s, :], corrected[:, s, :])
                    link(ins)
                    link(e.tensor_copy(rank[:, :, :], idx[:, :, :]))
                    for s in range(SUB):
                        ins = e.tensor_tensor(match[:, s, :, :],
                                              iota8[:, :].unsqueeze(2).broadcast_to([P, E, TOPK]),
                                              rank[:, s, 0:TOPK].unsqueeze(1).broadcast_to([P, E, TOPK]),
                                              ALU.is_equal)
                    link(ins)
                    link(e.tensor_reduce(chosen[:, :, :], match[:, :, :, :], AX, ALU.add))
                    link(e.tensor_tensor(kept[:, :, :], score[:, :, :], chosen[:, :, :], ALU.mult))
                    link(e.tensor_reduce(total[:, 2, :], kept[:, :, :], AX, ALU.add))
                    link(e.tensor_scalar(total[:, 2, :], total[:, 2, :], 1e-20, None, ALU.add))
                    link(e.reciprocal(total[:, 3, :], total[:, 2, :]))
                    link(e.scalar_tensor_tensor(gate[:, :, :], kept[:, :, :], tgw[:, 1:2],
                                                wide(total[:, 3, :].unsqueeze(2)), ALU.mult, ALU.mult))
                if kind == "fA":
                    j = st[3]
                    n = t.past("f_act", 1)
                    bk = f"F{j % 2}"
                    e.wait_ge(ev["f_th"], n)
                    if j >= 2:
                        e.wait_ge(ev["f_act"], t.past("f_act", -1))
                    link(e.scalar_tensor_tensor(th[:, j % 2, :], th[:, j % 2, :], 1.0, bank[bk][:, 0:TB],
                                                ALU.add, ALU.mult))
                    e.scalar_tensor_tensor(act_f[:, j % 2, :], th[:, j % 2, :], 0.5 / WS / WS,
                                           bank[bk][:, TB:2 * TB], ALU.mult, ALU.mult).then_inc(read[bk], 1)
                if kind == "fD":
                    j = st[3]
                    got("T1")
                    for s in range(SUB):
                        xs = x_sb[:, blk * SUB + s, :]
                        g = gate[:, s, j:j + 1] if j < E else tgw[:, 1:2]
                        ins = e.scalar_tensor_tensor(xs, bank["T1"][:, s * D:s * D + D], g, xs,
                                                     ALU.mult, ALU.add)
                    ins.then_inc(read["T1"], 1)
                    mine("T1")

            run(dve, handle)


CONSTS = {"ident": (P,), "zmask": (256,), "mask4": (4,), "mask8": (8,), "iota8": (E,),
          "g_all": (4,), "fm_rep": (16,), "fm_b": (1,), "sign": (1,), "b1": (1,), "b2": (E,), "bq": (KC,),
          "bkv": (2 * KC,), "rb": (1,), "ob": (2 * D,)}


def kernel(**inputs):
    import concourse.bacc as bacc
    from concourse.bass_utils import run_bass_kernel_spmd

    f = {k: np.ascontiguousarray(v) for k, v in inputs.items()}

    def rows(v):
        return np.ascontiguousarray(np.broadcast_to(v.reshape(1, -1), (P, v.size)))

    def cols(v):
        return np.ascontiguousarray(v.reshape(-1, P).T)

    p = np.arange(P)
    zmask = np.zeros((P, 2, 4, 2, 16), np.float32)
    for q in range(P):
        h = q // 16
        zmask[q, h // 4, h % 4, 0, :] = 1.0
        zmask[q, h // 4, h % 4, 1, :] = -1.0
    arrays = {
        "x": f["x"], "ctxT": np.ascontiguousarray(f["ctx_1024"].reshape(B * NK, D).T),
        "WqT": np.ascontiguousarray(f["L1_xattn_Wq"].T), "WkT": np.ascontiguousarray(f["L1_xattn_Wk"].T),
        "WvT": np.ascontiguousarray(f["L1_xattn_Wv"].T), "WoT": np.ascontiguousarray(f["L1_xattn_Wo"].T),
        "fcT": np.ascontiguousarray(f["L0_xattn_fc_w"].T), "expert_b": f["L0_ffn_expert_b"],
        "mask": rows(f["mask_BxS2_ik0"].astype(np.int32)).reshape(P, B, NK),
        "ident": np.eye(P, dtype=np.float32), "zmask": zmask.reshape(P, 256),
        "mask4": (p[:, None] // 32 == np.arange(4)).astype(np.float32),
        "mask8": (p[:, None] // 16 == np.arange(8)).astype(np.float32),
        "iota8": rows(np.arange(E, dtype=np.float32)),
        "g_all": rows(np.concatenate([f["g_xattn"], f["g_ffn"]])),
        "fm_rep": np.ascontiguousarray(np.tile(f["L0_xattn_fm_w"].T, (8, 1))), "fm_b": np.tile(f["L0_xattn_fm_b"], 8).reshape(P, 1),
        "sign": np.where(p % 32 < 16, 1.0, -1.0).astype(np.float32).reshape(P, 1),
        "b1": cols(f["L0_ffn_b1"]), "b2": rows(f["L0_ffn_b2"]), "bq": cols(f["L1_xattn_bq"]),
        "bkv": np.concatenate([cols(f["L1_xattn_bk"]), cols(f["L1_xattn_bv"])], axis=1),
        "rb": rows(f["L1_ffn_router_bias"].reshape(1)),
        "ob": rows(np.concatenate([f["L0_xattn_fc_b"], f["L1_xattn_bo"]])),
    }
    for n in ("L0_ffn_W1", "L0_ffn_W2", "L0_ffn_expert_W", "L1_ffn_router_w", "L1_ffn_gate_w", "L1_ffn_up_w",
              "L1_ffn_down_w", "L1_ffn_s_gate_w", "L1_ffn_s_up_w", "L1_ffn_s_down_w"):
        arrays[n] = f[n]
    nc = bacc.Bacc("TRN2", target_bir_lowering=False, num_devices=1)
    args = {}
    for n, v in arrays.items():
        v = arrays[n] = np.ascontiguousarray(v)
        args[n] = nc.dram_tensor("in_" + n, v.shape, mybir.dt.from_np(v.dtype), kind="ExternalInput").ap()
    args["out"] = nc.dram_tensor("out_x", (B * S, D), F32, kind="ExternalOutput").ap()
    gated_layers(nc, args)
    got = run_bass_kernel_spmd(nc, [{"in_" + n: v for n, v in arrays.items()}], core_ids=[0])
    return got.results[0]["out_x"].reshape(B, S, D)
```

```python
from contextlib import ExitStack

import numpy as np

import concourse.bass as bass
from concourse import mybir

F32 = mybir.dt.float32
F16 = mybir.dt.float16
BF16 = mybir.dt.bfloat16
I32 = mybir.dt.int32
U32 = mybir.dt.uint32
ALU = mybir.AluOpType
ACT = mybir.ActivationFunctionType
AX = mybir.AxisListType.X

P = 128
D = 256
KC = D // P
B = 4
S = 1024
NK = 77
H = 16
TB = 256
SUB = TB // P
NB = B * S // TB
BPB = S // TB
HK = H * NK
GW = HK // 4
NCH = (HK + P - 1) // P
HKP = NCH * P
HD = D // H
SPAN = 3
FIRST = [min(P * c // NK, H - SPAN) for c in range(NCH)]
E = 8
TOPK = 4
NI = 128
NSH = 4
WS = 16.0
EPS = 1e-5
FINITE_LOW = -1.0e30

BANKS = ("T0", "T1", "F0", "F1", "S0", "S1")


LAG = 2


def events(step):
    kind, layer, arg = step[0], step[1], step[3:]
    if kind == "aL":
        return {"a_stats": 1, "a_rstd": 1}
    if kind == "aM":
        return {"a_xn": 1, "a_xb": 1}
    if kind == "aX":
        return {"T0": 1, "a_xh": 1}
    if kind == "aZ":
        return {"T1": 1, "T0": 1} if layer == 0 else {"T1": 1, "a_qh": 1, "a_ql": 1}
    if kind == "aS":
        return {f"S{arg[0] % 2}": 1, "a_exp": 1}
    if kind == "aN":
        return {"a_rs": 1, "a_pn": 1}
    if kind == "aT":
        return {"T1": 1, "T0": 1}
    if kind == "aU":
        return {"T1": 1}
    if kind in ("aO", "aP"):
        return {"T0": 1}
    if kind == "aQ":
        return {"T1": 1, "a_vh": 1}
    if kind == "fL":
        return {"f_stats": 1, "f_rstd": 1}
    if kind == "fN":
        return {"f_xn": 1}
    if kind == "fX":
        return {"T1": 1, "f_xh": 1}
    if kind == "fH":
        return {"T0": 1, "f_hs": 1}
    if kind == "fM":
        return {"T1": 1, "f_gate": 1}
    if kind == "fB":
        return {"T0": 1, "T1": 1, "f_add0": 1}
    if kind == "fE":
        return {f"F{arg[0] % 2}": 1, f"f_add{arg[0] % 2}": 1}
    if kind == "fR":
        return ({"T0": 1, "f_nmx": 1}, {"f_re": 1}, {}, {"f_gate": 1})[arg[0]]
    if kind == "fG":
        return {f"F{arg[0] % 2}": 1, "f_th": 1}
    if kind == "fA":
        return {"f_ah": 1, "f_act": 1}
    if kind == "fD":
        return {"T1": 1, "f_used": 1 if arg[0] < E else NSH, f"f_add{arg[0] % 2}": 1}
    if kind == "pF":
        return {"T0": 2, "T1": 2}
    if kind == "pV":
        return {"p_kv": 1}
    if kind == "pW":
        return {"T0": NCH // 2, "T1": NCH // 2}
    if kind in ("out", "split", "loaded", "pK", "pC", "pZ", "kv"):
        return {}
    raise ValueError(kind)


ORDERS = (
    {
        "PE":
        "E:2 L N0 S0 S1 E:0 S2 N1 E:3 S3 B: M E:4 T0 fL E:5 X U0 E:6 N2 O0 E:7 N3 fN Z fX +H: T1 U1 O1 "
        "+M: +E:1",
        "ACT":
        "E:2 S0 E:0 L S1 M E:3 fL N0 N1 B: fN S2 N2 N3 T0 E:4 X U0 O0 E:5 S3 Z fX +H: T1 U1 E:6 E:7 +M: "
        "O1 +E:1",
        "DVE":
        "E:2 L S0 E:0 E:3 B: S1 N0 N1 E:5 S2 fL M T0 N2 S3 U0 E:4 X E:6 O0 N3 fN E:7 Z fX +H: T1 U1 O1 "
        "+M: +E:1",
        "POOL":
        "E:2 L E:0 N0 S0 N1 S1 B: S2 E:3 E:4 M N2 T0 fL U0 X N3 fN E:5 O0 S3 E:6 E:7 Z fX +H: T1 U1 +M: "
        "O1 +E:1",
    },
    {
        "PE":
        "G:3 L A:3 S0 D:1 S1 G:4 D:2 G:5 S2 D:3 A:4 A:5 N0 G:6 N1 A:6 fL T0 D:4 G:7 N2 M U0 G:8 D:5 A:7 "
        "S3 fN P0 D:6 G:9 A:8 N3 A:9 Q0 X G:10 D:7 T1 U1 A:10 G:11 O0 A:11 fX +R:0 +G:0 +R:1 P1 D:8 +A:0 "
        "+R:2 +G:1 Q1 +G:2 out: +A:1 Z +R:3 O1 +D:0 +A:2",
        "ACT":
        "G:3 D:1 A:3 S0 L G:4 D:2 A:4 N0 S1 N1 G:5 D:3 A:5 G:6 T0 D:4 A:6 fL G:7 U0 S2 A:7 P0 D:5 G:8 D:6 "
        "N2 M fN G:9 S3 Q0 A:8 N3 X D:7 G:10 A:9 T1 U1 G:11 A:10 fX +G:0 O0 +R:0 A:11 +R:1 +R:2 D:8 +A:0 "
        "+G:1 P1 Q1 out: +A:1 +G:2 Z +R:3 +D:0 +A:2 O1",
        "DVE":
        "G:3 L G:4 A:3 S0 D:1 D:2 G:5 S1 A:4 G:6 N0 N1 D:3 G:7 A:5 fL T0 D:4 A:6 M G:8 S2 U0 G:9 A:7 fN "
        "A:8 P0 D:5 S3 N2 D:6 A:9 Q0 X G:10 G:11 A:10 D:7 T1 U1 A:11 O0 fX +G:0 +R:0 N3 +G:1 +R:1 +R:2 "
        "D:8 +A:0 P1 Q1 +G:2 out: +A:1 +R:3 Z +A:2 +D:0 O1",
        "POOL":
        "G:3 A:3 S0 G:4 D:1 L G:5 A:4 G:6 N0 S1 N1 D:2 D:3 M A:5 T0 A:6 fL D:4 G:7 G:8 A:7 U0 fN D:5 P0 "
        "D:6 X G:9 N2 N3 Q0 D:7 T1 S2 A:8 G:10 O0 A:9 A:10 U1 fX S3 G:11 +G:0 +G:1 +R:0 +R:1 A:11 +R:2 P1 "
        "D:8 +A:0 Q1 +R:3 +G:2 out: +A:1 O1 Z +A:2 +D:0",
    },
)


IRREGULAR = {
    0:
        "S0 S1 S2 S3 pW/0/1 N0 L M N1 split/0/0 X split/0/1 pV/0/2 T0 Z U0 pW/0/2 split/0/2 N2 N3 "
        "split/0/3 O0 pV/0/3 split/0/4 split/0/5 T1 U1 split/0/6 O1",
    1:
        "split/0/7 split/0/8 S0 S1 S2 L M pW/0/3 N0 N1 X fL T0 U0 fN N2 split/0/9 kv/0 S3 O0 fX "
        "loaded/0/1 split/0/10 pF/1 Z N3 split/0/11 split/0/12 +H: T1 U1 split/0/13 split/0/14 split/0/15 "
        "split/0/16 O1 +M: split/0/17 +E:1",
    NB - 1:
        "fL E:2 S0 B: N0 L S1 S2 N1 E:0 E:3 E:4 E:5 M T0 N2 fN pC/1 U0 S3 X E:6 N3 pV/1/0 E:7 O0 fX +H: "
        "T1 U1 Z O1 pW/1/0 +M: +E:1",
    NB:
        "loaded/0/2 pZ/1 L S0 S1 E:2 fL pV/1/1 N0 B: N1 M E:0 S2 T0 E:3 fN U0 S3 E:4 E:5 P0 pW/1/1 N2 E:6 "
        "X N3 E:7 fX Q0 Z O0 pV/1/2 +H: T1 U1 P1 Q1 O1 +M: +E:1",
    NB + 1:
        "S0 fL S1 N0 E:2 B: N1 E:0 T0 U0 L M E:3 fN pW/1/2 X S2 E:4 S3 N2 P0 N3 E:5 pV/1/3 E:6 T1 U1 E:7 "
        "fX pW/1/3 P1 Q0 O0 Q1 O1 +R:0 +G:0 +R:1 +A:0 +R:2 Z +G:1 +G:2 +A:1 +R:3 +D:0 +A:2",
    2 * NB:
        "G:3 G:4 A:3 fL D:1 G:5 A:4 G:6 D:2 A:5 A:6 G:7 D:3 D:4 G:8 A:7 D:5 A:8 G:9 D:6 A:9 G:10 A:10 "
        "G:11 D:7 fN A:11 fX D:8 out: +R:0 +G:0 +R:1 +A:0 +R:2 +G:1 +G:2 +A:1 +R:3 +D:0 +A:2",
    2 * NB + 1:
        "G:3 G:4 A:3 D:1 G:5 A:4 D:2 G:6 A:5 D:3 A:6 G:7 A:7 G:8 D:4 G:9 A:8 D:5 G:10 A:9 D:6 A:10 G:11 "
        "A:11 D:7 D:8 out:",
}


def ffn_steps(layer):
    if layer == 0:
        return ["H:", "M:", "B:"] + [f"E:{e}" for e in range(E)]
    out, nj = [], E + NSH
    for j in range(nj + 2):
        out += [f"G:{j}"] if j < nj else []
        out += [f"A:{j - 1}"] if 1 <= j <= nj else []
        out += [f"D:{j - 2}"] if 2 <= j < E + 2 else []
        out += [f"R:{i}" for i in range(4)] if j == 1 else []
    return out + [f"D:{E}", "out:"]


def ffn_step(name, f):
    kind, args = name.split(":")
    return ("out" if kind == "out" else "f" + kind, *f, *(int(v) for v in args.split(",") if v))


def round_steps(att, ffn, next_att, next_ffn, order):
    out = []
    for w in order:
        if "/" in w:
            kind, layer, *args = w.split("/")
            out.append((kind, int(layer), 0, *(int(v) for v in args)))
        elif w[0] == "+":
            out += [ffn_step(w[1:], next_ffn)] if next_ffn else []
        elif ":" in w:
            out += [ffn_step(w, ffn)] if ffn else []
        elif w[0] == "f":
            out += [(w, *next_ffn)] if next_ffn else []
        elif w in ("L", "M", "X", "Z"):
            out += [("a" + w, *next_att)] if next_att else []
        elif att is not None:
            out.append(("a" + w[0], *att, int(w[1])))
    return out


class Tally:

    def __init__(self):
        self.n, self.rate, self.it, self.batch = {}, {}, None, 0

    def past(self, name, more=0):
        n = self.n.get(name, 0) + more
        if self.it is None:
            return n
        return self.it * self.rate.get(name, 0) + n

    def step(self, names):
        for k, v in names.items():
            self.n[k] = self.n.get(k, 0) + v

    def enter(self, it, rate):
        self.it, self.rate = it, rate

    def leave(self, trips):
        self.it = None
        for k, v in self.rate.items():
            self.n[k] = self.n.get(k, 0) + v * (trips - 1)


class Dry:

    def __getattr__(self, name):
        return lambda *a, **k: self


def gated_layers(nc, a):
    with ExitStack() as ctx:
        def sb(name, shape, dt=F32):
            return ctx.enter_context(nc.sbuf_tensor(name, shape, dt))

        def pb(name, shape):
            return ctx.enter_context(nc.psum_tensor(name, shape, F32))

        x_sb = sb("x_sb", [P, NB * SUB, D])
        ctx_t = sb("ctx_t", [P, KC, B * NK])
        th_act = sb("th_act", [P, 4, TB])
        th, act_f = th_act[:, 0:2, :], th_act[:, 2:4, :]
        h_t = th_act[:, 0, :]
        fo_w = th_act
        k_bd = sb("k_bd", [P, B, HK])
        w_vo = sb("w_vo", [P, B, NCH, D])
        stage = x_sb[:, NB * SUB // 2:, :].rearrange("p t d -> p (t d)").rearrange("p (a n) -> p a n", a=2)
        l1 = w_vo[:, :, :, :].rearrange("p b c d -> p (b c d)")
        diff = l1[:, 0:4 * GW].rearrange("p (u c) -> p u c", u=2)
        n0 = 4 * GW
        n1 = n0 + B * NCH * SPAN * (HD + 1)
        v_rows = l1[:, n0:n1].bitcast(F16).rearrange("p (w b c n) -> p w b c n", w=2, b=B, c=NCH)
        v_t = l1[:, n1:n1 + D].bitcast(F16).rearrange("p (w c t) -> p w c t", w=2, c=KC)
        k16 = k_bd[:, :, :].bitcast(F16).rearrange(
            "p b (w c) -> p b w c", w=2)
        n2 = n1 + D
        n3 = n2 + 4 * B * NK
        n4 = n3 + 2 * (2 * GW + 2 * P)
        feat16 = l1[:, n2:n3].bitcast(F16).rearrange("p (w g c) -> p w g c", w=2, g=4)
        padded16 = l1[:, n3:n4].bitcast(F16).rearrange("p (w g c) -> p w g c", w=2, g=2)
        zero16 = l1[:, n4:n4 + 256].bitcast(F16)
        scaled1 = l1[:, n4 + 256:n4 + 256 + 4 * D].rearrange("p (a s n) -> p a s n", a=2, s=SUB)
        probs = sb("probs", [P, SUB, HKP])
        probs16 = probs[:, :, :].bitcast(F16).rearrange("p s (w c) -> p s w c", w=2)
        probs_t = sb("probs_t", [P, NCH, P])
        probs_t16 = probs_t[:, :, :].bitcast(F16).rearrange("p c (w t) -> p c w t", w=2)
        q_t = sb("q_t", [P, 4, TB])
        q16 = q_t[:, 2:4, :].rearrange("p a t -> p (a t)").bitcast(F16).rearrange(
            "p (w c t) -> p w c t", w=2, c=KC)
        mv = sb("mv", [P, 2, SUB, 2])
        stats = sb("stats", [P, 2, SUB, 6])
        rstd = sb("rstd", [P, 2, SUB])
        xn = sb("xn", [P, 2, SUB, D])
        xh = sb("xh", [P, 2, KC, TB], F16)
        xl = sb("xl", [P, 2, KC, TB], F16)
        row_max = sb("row_max", [P, 2, 8])
        head_inv = sb("head_inv", [P, H])
        row_inv = sb("row_inv", [P, 2, 2, 8])
        h_hi = sb("h_hi", [P, TB], F16)
        h_lo = sb("h_lo", [P, TB], F16)
        one_hot = sb("one_hot", [P, SUB, P], F16)
        one_hot_t = sb("one_hot_t", [P, SUB, P], F16)
        gate = sb("gate", [P, SUB, E])
        logits, top, shifted, expo, score, corrected, rank, chosen, kept = (
            sb(n, [P, SUB, E]) for n in ("logits", "top", "shifted", "expo", "score", "corrected", "rank",
                                         "chosen", "kept"))
        match = sb("match", [P, SUB, E, TOPK])
        total = sb("total", [P, 4, SUB])
        unused = sb("unused", [P, 1])
        unused_pool = sb("unused_pool", [P, 1])
        idx = sb("idx", [P, SUB, 8], U32)
        act = sb("act", [P, 2, E + NSH, TB], F16)
        padded = act[:, :, :, :].rearrange("p a j t -> p (a j t)").bitcast(F32)[
            :, 0:4 * (GW + 2 * P)].rearrange("p (g c) -> p g c", g=4)
        scaled0 = act[:, 1, :, :].rearrange("p j t -> p (j t)")[:, (E + NSH) * TB - 8 * D:].bitcast(F32).rearrange(
            "p (a s n) -> p a s n", a=2, s=SUB)
        scaled = (scaled0, scaled1)
        act_32 = act[:, :, :, :].rearrange("p a j t -> p (a j t)").bitcast(F32)
        kv_w = act_32[:, 0:4 * D].rearrange("p (a c n) -> p a c n", a=2, c=KC)
        feat1 = [act_32[:, 4 * D + g * B * NK:4 * D + (g + 1) * B * NK] for g in range(3)]
        feat1.append(sb("feat_last", [P, B * NK])[:, :])
        feat = probs[:, :, :].rearrange("p s c -> p (s c)")[:, 0:4 * B * NK].rearrange(
            "p (g c) -> p g c", g=4)
        zw32 = sb("zw32", [P, 2, P])
        mask_i = xn[:, 1, :, :].rearrange("p s d -> p (s d)")[:, 0:B * NK].rearrange(
            "p (b k) -> p b k", b=B).bitcast(I32)
        mask_low = sb("mask_low", [P, B, GW], BF16)
        share = sb("share", [P, P], BF16)
        x_bias = sb("x_bias", [P, 2, D])
        tg = sb("tg", [P, 4])
        tgx = sb("tgx", [P, 1])
        tgw = sb("tgw", [P, 2])
        eps_t = sb("eps_t", [P, SUB])
        rs_exp = sb("rs_exp", [P, SUB])

        consts = {}
        consts["zmask"] = xn[:, 0, 0, :]
        consts["ob"] = q_t[:, 0:2, :].rearrange("p a n -> p (a n)")
        for name, shape in CONSTS.items():
            if name in consts:
                continue
            consts[name] = sb("c_" + name, [P] + list(shape))
        ident, zmask, mask4, mask8, iota8 = (consts[n] for n in ("ident", "zmask", "mask4", "mask8", "iota8"))
        ident16 = sb("ident16", [P, P], F16)

        def split(name, shape):
            return sb(name + "_h", [P] + shape, F16), sb(name + "_l", [P] + shape, F16)

        zw = split("zw", [2, P])
        w1 = split("w1", [KC, P])
        w2 = split("w2", [E])
        ew = split("ew", [KC, E, D])
        eb = split("eb", [D])
        wq = split("wq", [KC, D])
        wo = split("wo", [KC, D])
        rw = split("rw", [KC, E])
        gw = split("gw", [KC, E + NSH, NI])
        uw = split("uw", [KC, E + NSH, NI])
        dw = split("dw", [E + NSH, D])

        bank = {n: pb("ps_" + n, [P, 512]) for n in ("T0", "T1", "F0", "F1")}
        bank["S0"] = pb("ps_S0", [P, 2, 512])
        bank["S1"] = pb("ps_S1", [P, 2, 512])

        def sem(name):
            return ctx.enter_context(nc.semaphore(name))

        filled = {n: sem("filled_" + n) for n in BANKS}
        read = {n: sem("read_" + n) for n in BANKS}
        ev = {n: sem(n) for n in (
            "a_stats", "a_rstd", "a_xn", "a_xb", "a_xh", "a_qh", "a_ql", "a_vh", "a_exp", "a_rs", "a_pn",
            "f_stats", "f_rstd", "f_xn", "f_xh", "f_hs", "f_gate", "f_nmx", "f_re",
            "f_th", "f_ah", "f_act", "f_add0", "f_add1", "p_kv")}
        first_in = sem("first_in")
        small_in = sem("small_in")
        x_in = sem("x_in")
        x_late_in = sem("x_late_in")
        stage_in = [sem("stage_in0"), sem("stage_in1")]
        split_hi = sem("split_hi")
        split_lo = sem("split_lo")
        ready = sem("ready")
        tanh_done = sem("tanh_done")
        kv_in = sem("kv_in")
        out_done = sem("out_done")
        dve_seq = sem("dve_seq")
        pool_seq = sem("pool_seq")

        def part(src, pair, sl):
            return src, sl(pair[0]), sl(pair[1])

        def kcn(w):
            return w.rearrange("(c p) n -> p c n", p=P)

        pieces = [part(kcn(a["L0_ffn_W1"]), w1, lambda t: t[:, :, :]),
                  part(a["L0_ffn_W2"], w2, lambda t: t[:, :])]
        for c in range(KC):
            src = a["L0_ffn_expert_W"].rearrange("e (c p) n -> c p e n", p=P)[c]
            pieces.append(part(src, ew, lambda t, c=c: t[:, c, :, :]))
        pieces += [part(a["expert_b"], eb, lambda t: t[:, :]),
                   part(kcn(a["WqT"]), wq, lambda t: t[:, :, :]),
                   part(kcn(a["WoT"]), wo, lambda t: t[:, :, :]),
                   part(kcn(a["L1_ffn_router_w"]), rw, lambda t: t[:, :, :])]
        for nm, sh, w in (("gate_w", "s_gate_w", gw), ("up_w", "s_up_w", uw)):
            for c in range(KC):
                src = a["L1_ffn_" + nm].rearrange("e (c p) n -> c p e n", p=P)[c]
                pieces.append(part(src, w, lambda t, c=c: t[:, c, 0:E, :]))
                src = a["L1_ffn_" + sh].rearrange("(c p) (j n) -> c p j n", p=P, n=NI)[c]
                pieces.append(part(src, w, lambda t, c=c: t[:, c, E:E + NSH, :]))
        pieces.append(part(a["L1_ffn_down_w"].rearrange("e p n -> p e n"), dw, lambda t: t[:, 0:E, :]))
        pieces.append(part(a["L1_ffn_s_down_w"].rearrange("(j p) n -> p j n", p=P), dw,
                           lambda t: t[:, E:E + NSH, :]))

        def staged(k, like):
            n = int(np.prod(like.shape[1:]))
            v = stage[:, k % 2, 0:n]
            if len(like.shape) == 3:
                v = v.rearrange("p (a b) -> p a b", b=like.shape[2])
            return v

        n_first = 5
        names = list(CONSTS)
        first_loads = [(consts[n], a[n]) for n in names[:n_first]]
        first_loads.append((ctx_t, a["ctxT"].rearrange("(c p) n -> p c n", p=P)))
        small_loads = [(consts[n], a[n]) for n in names[n_first:]]
        small_loads += [(fo_w, a["fcT"].rearrange("(g p) n -> p g n", p=P)), (mask_i, a["mask"])]
        n_pieces0 = 5

        def prog(walk, who):
            def steps(k):
                def rel(j):
                    return (j // NB, j % NB - k % NB) if 0 <= j < 2 * NB else None
                order = IRREGULAR[k] if k in IRREGULAR else ORDERS[k // NB][who]
                return round_steps(rel(k), rel(k - LAG), rel(k + 1), rel(k + 1 - LAG), order.split())

            walk([("pF", 0, 0), ("pV", 0, 0, 0), ("pW", 0, 0, 0),
                  ("loaded", 0, 0, 0), ("aL", 0, 0), ("aM", 0, 0), ("pK", 0, 0),
                  ("pV", 0, 0, 1), ("aX", 0, 0), ("aZ", 0, 0)], 0)
            for layer in range(2):
                k0 = layer * NB
                for k in range(LAG):
                    walk(steps(k0 + k), k)
                for b in range(B):
                    first, end = max(LAG, b * BPB), min(NB - 1, (b + 1) * BPB)
                    walk(steps(k0 + first), first, trips=end - first)
                walk(steps(k0 + NB - 1), NB - 1)
            for k in range(2 * NB, 2 * NB + LAG):
                walk(steps(k), k % NB)

        def run(eng, handle, who):
            t = Tally()

            def walk(steps, rnd, trips=None):
                t.batch = rnd // BPB
                def body(e, i):
                    for st in steps:
                        handle(e, t, st, rnd + st[2] if i is None else i + (rnd + st[2]))
                        t.step(events(st))

                if trips is None:
                    body(eng, None)
                    return
                before = dict(t.n)
                body(Dry(), 0)
                rate = {k: v - before.get(k, 0) for k, v in t.n.items()}
                t.n = before
                with eng.Fori(0, trips) as i:
                    t.enter(i, rate)
                    body(eng, i)
                t.leave(trips)

            prog(walk, who)

        def at_least(e, s, n):
            if not (isinstance(n, int) and n <= 0):
                e.wait_ge(s, n)

        block = ctx.enter_context(nc.Block())

        @block.sync
        def _(sp):
            for loads, s_ in ((first_loads, first_in), (small_loads, small_in)):
                for dst, src in loads:
                    sp.dma_start(dst[tuple([slice(None)] * len(dst.shape))], src).then_inc(s_, 16)
            for b in range(B // 2):
                sp.dma_start(x_sb[:, b * 8:(b + 1) * 8, :],
                             a["x"][b].rearrange("(t p) d -> p t d", p=P)).then_inc(x_in, 16)
            for k, (src, hi, _) in enumerate(pieces):
                if k >= 2:
                    sp.wait_ge(split_lo, k - 1)
                np_ = src.shape[0]
                sp.dma_start(staged(k, hi)[0:np_], src).then_inc(stage_in[k % 2], 16)
            sp.wait_ge(split_lo, len(pieces))
            for b in range(B // 2, B):
                sp.dma_start(x_sb[:, b * 8:(b + 1) * 8, :],
                             a["x"][b].rearrange("(t p) d -> p t d", p=P)).then_inc(x_late_in, 16)

            def handle(e, t, st, blk):
                if st[0] == "out":
                    e.wait_ge(ev["f_add0"], t.past("f_add0"))
                    dst = a["out"].rearrange("(t p) d -> p t d", p=P)
                    e.dma_start(dst[:, bass.ts(blk, SUB), :],
                                x_sb[:, bass.ts(blk, SUB), :]).then_inc(out_done, 16)

            run(sp, handle, "PE")
            sp.wait_ge(out_done, 16 * NB)

        @block.tensor
        def _(pe):
            def mm3(e, out, lh, ll, rh, rl, first, last):
                e.matmul(out, lh, rh, start=first, stop=False)
                e.matmul(out, lh, rl, start=False, stop=False)
                return e.matmul(out, ll, rh, start=False, stop=last)

            def handle(e, t, st, blk):
                kind, layer = st[0], st[1]
                batch = t.batch

                def take(name, use=0):
                    at_least(e, read[name], t.past(name, use))

                if kind == "pF":
                    if layer == 0:
                        e.wait_ge(ready, 1)
                    else:
                        e.wait_ge(kv_in, 32)
                    for g in range(4):
                        bk = f"T{g % 2}"
                        take(bk, g // 2)
                        o = bank[bk][:, 0:B * NK]
                        if layer == 0:
                            mm = e.matmul(o, zw32[:, g % 2, :], ctx_t[:, g // 2, :], start=True, stop=True)
                        else:
                            for c in range(KC):
                                mm = e.matmul(o, kv_w[:, g // 2, c, (g % 2) * P:(g % 2) * P + P],
                                              ctx_t[:, c, :], start=(c == 0), stop=(c == KC - 1))
                        mm.then_inc(filled[bk], 1)
                if kind == "loaded" and st[3] > 0:
                    e.wait_ge(split_lo, n_pieces0 if st[3] == 1 else len(pieces))
                if kind == "pW":
                    if layer == 0 and st[3] == 0:
                        e.wait_ge(ready, 2)
                        e.wait_ge(small_in, 16 * len(small_loads))
                    e.wait_ge(ev["p_kv"], t.past("p_kv"))
                    for c in range(NCH):
                        bk = f"T{c % 2}"
                        take(bk, c // 2)
                        if layer == 1:
                            for g in range(2):
                                for w in range(2):
                                    if any(h // 8 == g for h in range(FIRST[c], FIRST[c] + SPAN)):
                                        at = min(max(P + P * c - 2 * GW * g, 0), 2 * GW + P)
                                        o = bank[bk][:, (2 * w + g) * (P // 2):(2 * w + g + 1) * (P // 2)]
                                        mm = e.transpose(o.bitcast(F16), padded16[:, w, g, at:at + P],
                                                         ident16[:, :])
                            mm.then_inc(filled[bk], 1)
                            continue
                        gs = [g for g in range(4) if P * c < GW * (g + 1) and P * (c + 1) > GW * g]
                        for g in gs:
                            at = P + P * c - GW * g
                            mm = e.matmul(bank[bk][:, 0:D], padded[:, g, at:at + P], fo_w[:, g, :],
                                          start=(g == gs[0]), stop=(g == gs[-1]))
                        mm.then_inc(filled[bk], 1)
                if kind in ("aX", "fX"):
                    w = 0 if kind == "aX" else 1
                    bk = "T0" if w == 0 else "T1"
                    e.wait_ge(ev["a_xn" if w == 0 else "f_xn"], t.past("a_xn" if w == 0 else "f_xn"))
                    take(bk)
                    for c in range(KC):
                        for s in range(SUB):
                            mm = e.transpose(bank[bk][:, c * TB + s * P:c * TB + s * P + P],
                                             xn[:, w, s, c * P:c * P + P], ident[:, :])
                    mm.then_inc(filled[bk], 1)
                if kind == "aZ":
                    e.wait_ge(read["T0"], t.past("T0"))
                    for o4 in range(4 if layer == 0 else KC):
                        bk = f"T{1 - o4 // 2}"
                        if o4 % 2 == 0:
                            take(bk)
                        o = bank[bk][:, (o4 % 2) * TB:(o4 % 2) * TB + TB]
                        if layer == 0:
                            mm = mm3(e, o, zw[0][:, o4 % 2, :], zw[1][:, o4 % 2, :],
                                     xh[:, 0, o4 // 2, :], xl[:, 0, o4 // 2, :], True, True)
                        else:
                            for c in range(KC):
                                cols = slice(o4 * P, o4 * P + P)
                                mm = mm3(e, o, wq[0][:, c, cols], wq[1][:, c, cols], xh[:, 0, c, :],
                                         xl[:, 0, c, :], c == 0, c == KC - 1)
                        if o4 % 2 == 1:
                            mm.then_inc(filled[bk], 1)
                if kind == "aS":
                    u = st[3]
                    s, half = u // 2, u % 2
                    bk = f"S{u % 2}"
                    if u == 0:
                        e.wait_ge(read["T1"], t.past("T1"))
                        e.wait_ge(read["T0"], t.past("T0"))
                    take(bk)
                    if layer == 1 and u == 0:
                        e.wait_ge(ev["a_ql"], t.past("a_ql"))
                    for gg in range(2):
                        at = (2 * half + gg) * GW
                        o = bank[bk][:, gg, 0:GW]
                        if layer == 0:
                            mm = e.matmul(o, q_t[:, 2 * half + gg, s * P:s * P + P],
                                          k_bd[:, batch, at:at + GW], start=True, stop=True)
                        else:
                            mm3(e, o, q16[:, 0, half, s * P:s * P + P], q16[:, 1, half, s * P:s * P + P],
                                k16[:, batch, 0, at:at + GW], k16[:, batch, 1, at:at + GW],
                                True, False)
                            mm = e.matmul(o, share[:, :], mask_low[:, batch, :], start=False, stop=True)
                    mm.then_inc(filled[bk], 1)
                if kind in ("aT", "aU"):
                    s = st[3]
                    if kind == "aT":
                        e.wait_ge(ev["a_pn"], t.past("a_pn"))
                    for piece, bk in ((0, "T1"), (1, "T0")) if kind == "aT" else ((2, "T1"),):
                        take(bk)
                        for c in range(4 * piece, min(4 * piece + 4, NCH)):
                            if layer == 0:
                                mm = e.transpose(bank[bk][:, (c % 4) * P:(c % 4) * P + P],
                                                 probs[:, s, c * P:c * P + P], ident[:, :])
                                continue
                            for w in range(2):
                                at = (c % 4) * P + w * (P // 2)
                                mm = e.transpose(bank[bk][:, at:at + P // 2].bitcast(F16),
                                                 probs16[:, s, w, c * P:c * P + P], ident16[:, :])
                        mm.then_inc(filled[bk], 1)
                if kind == "aP":
                    e.wait_ge(read["T0"], t.past("T0"))
                    e.wait_ge(read["T1"], t.past("T1"))
                    e.matmul(bank["T0"][:, 0:H * (HD + 1)], zero16[:, 0:P], zero16[:, 0:H * (HD + 1)],
                             start=True, stop=False)
                    for c in range(NCH):
                        o = bank["T0"][:, FIRST[c] * (HD + 1):(FIRST[c] + SPAN) * (HD + 1)]
                        vh, vl = (v_rows[:, w, batch, c, :] for w in range(2))
                        mm = mm3(e, o, probs_t16[:, c, 0, :], probs_t16[:, c, 1, :], vh, vl,
                                 False, c == NCH - 1)
                    mm.then_inc(filled["T0"], 1)
                if kind == "aQ":
                    s = st[3]
                    e.wait_ge(read["T0"], t.past("T0"))
                    take("T1")
                    for c in range(KC):
                        mm = e.transpose(bank["T1"][:, c * P:c * P + P], probs[:, s, c * P:c * P + P],
                                         ident[:, :])
                    mm.then_inc(filled["T1"], 1)
                if kind == "aO" and layer == 1:
                    e.wait_ge(read["T1"], t.past("T1"))
                    take("T0")
                    for c in range(KC):
                        mm = mm3(e, bank["T0"][:, 0:D], v_t[:, 0, c, :], v_t[:, 1, c, :], wo[0][:, c, :],
                                 wo[1][:, c, :], c == 0, c == KC - 1)
                    mm.then_inc(filled["T0"], 1)
                if kind == "aO" and layer == 0:
                    e.wait_ge(read["T0"], t.past("T0"))
                    e.wait_ge(read["T1"], t.past("T1"))
                    for c in range(NCH):
                        mm = e.matmul(bank["T0"][:, 0:D], probs_t[:, c, :], w_vo[:, batch, c, :],
                                      start=(c == 0), stop=(c == NCH - 1))
                    mm.then_inc(filled["T0"], 1)
                if kind == "fH":
                    e.wait_ge(read["T1"], t.past("T1"))
                    take("T0")
                    for c in range(KC):
                        mm = mm3(e, bank["T0"][:, 0:TB], w1[0][:, c, :], w1[1][:, c, :],
                                 xh[:, 1, c, :], xl[:, 1, c, :], c == 0, c == KC - 1)
                    mm.then_inc(filled["T0"], 1)
                if kind == "fM":
                    e.wait_ge(ev["f_hs"], t.past("f_hs"))
                    take("T1")
                    for s in range(SUB):
                        tok = slice(s * P, s * P + P)
                        mm = mm3(e, bank["T1"][:, s * E:s * E + E], h_hi[:, tok], h_lo[:, tok],
                                 w2[0][:, :], w2[1][:, :], True, True)
                    mm.then_inc(filled["T1"], 1)
                if kind == "fB":
                    e.wait_ge(read["T1"], t.past("T1"))
                    take("T0")
                    for s in range(SUB):
                        mm = e.transpose(bank["T0"][:, s * (P // 2):(s + 1) * (P // 2)].bitcast(F16),
                                         one_hot[:, s, :], ident16[:, :])
                    mm.then_inc(filled["T0"], 1)
                    e.wait_ge(read["T0"], t.past("T0", 1))
                    take("T1")
                    for s in range(SUB):
                        o = bank["T1"][:, s * D:s * D + D]
                        e.matmul(o, one_hot_t[:, s, :], eb[0][:, :], start=True, stop=False)
                        mm = e.matmul(o, one_hot_t[:, s, :], eb[1][:, :], start=False, stop=True)
                    mm.then_inc(filled["T1"], 1)
                if kind == "fE":
                    j = st[3]
                    bk = f"F{j % 2}"
                    take(bk)
                    for s in range(SUB):
                        tok = slice(s * P, s * P + P)
                        for c in range(KC):
                            mm = mm3(e, bank[bk][:, s * D:s * D + D], xh[:, 1, c, tok], xl[:, 1, c, tok],
                                     ew[0][:, c, j, :], ew[1][:, c, j, :], c == 0, c == KC - 1)
                    mm.then_inc(filled[bk], 1)
                if kind == "fR" and st[3] == 0:
                    e.wait_ge(read["T1"], t.past("T1"))
                    take("T0")
                    for s in range(SUB):
                        tok = slice(s * P, s * P + P)
                        for c in range(KC):
                            mm = mm3(e, bank["T0"][:, s * E:s * E + E], xh[:, 1, c, tok], xl[:, 1, c, tok],
                                     rw[0][:, c, :], rw[1][:, c, :], c == 0, c == KC - 1)
                    mm.then_inc(filled["T0"], 1)
                if kind == "fG":
                    j = st[3]
                    bk = f"F{j % 2}"
                    if j == 0:
                        e.wait_ge(read["T1"], t.past("T1"))
                    take(bk)
                    for m, w in enumerate((gw, uw)):
                        for c in range(KC):
                            mm = mm3(e, bank[bk][:, m * TB:m * TB + TB], w[0][:, c, j, :],
                                     w[1][:, c, j, :], xh[:, 1, c, :], xl[:, 1, c, :],
                                     c == 0, c == KC - 1)
                    mm.then_inc(filled[bk], 1)
                if kind == "fD":
                    j = st[3]
                    js = [j] if j < E else list(range(E, E + NSH))
                    e.wait_ge(ev["f_act"], t.past("f_used", len(js)))
                    take("T1")
                    for s in range(SUB):
                        tok = slice(s * P, s * P + P)
                        for jj in js:
                            mm = mm3(e, bank["T1"][:, s * D:s * D + D], act[:, 0, jj, tok],
                                     act[:, 1, jj, tok], dw[0][:, jj, :], dw[1][:, jj, :],
                                     jj == js[0], jj == js[-1])
                    mm.then_inc(filled["T1"], 1)

            run(pe, handle, "PE")

        @block.scalar
        def _(sc):
            sc.wait_ge(first_in, 16 * len(first_loads))
            sc.activation(tg[:, :], consts["g_all"][:, :], ACT.Tanh).then_inc(tanh_done, 1)

            def handle(e, t, st, blk):
                kind, layer = st[0], st[1]

                def got(name, use=0):
                    e.wait_ge(filled[name], t.past(name, use + 1))

                if kind == "kv":
                    e.wait_ge(read["T0"], t.past("T0"))
                    e.wait_ge(read["T1"], t.past("T1"))
                    e.dma_start(kv_w[:, 0], kcn(a["WkT"])).then_inc(kv_in, 16)
                    e.dma_start(kv_w[:, 1], kcn(a["WvT"])).then_inc(kv_in, 16)
                if kind == "split":
                    k = st[3]
                    src, hi, _ = pieces[k]
                    e.wait_ge(stage_in[k % 2], 16 * (k // 2 + 1))
                    np_ = src.shape[0]
                    e.activation(hi[0:np_], staged(k, hi)[0:np_], ACT.Copy, scale=WS).then_inc(split_hi, 1)
                if kind == "pF":
                    if layer == 0:
                        e.wait_ge(ready, 1)
                    for g in range(4):
                        bk = f"T{g % 2}"
                        got(bk, g // 2)
                        if layer == 0:
                            e.activation(feat[:, g, :], bank[bk][:, 0:B * NK], ACT.Exp,
                                         bias=consts["fm_b"][:, 0:1]).then_inc(read[bk], 1)
                        else:
                            bias = consts["bkv"][:, g:g + 1]
                            e.activation(feat1[g], bank[bk][:, 0:B * NK], ACT.Identity,
                                         bias=bias).then_inc(read[bk], 1)
                if kind == "pW":
                    b = st[3]
                    for c in range(NCH):
                        bk = f"T{c % 2}"
                        got(bk, c // 2)
                        if layer == 1:
                            both = bank[bk][:, 0:2 * P].bitcast(F16).rearrange("p (w g f) -> p w g f", w=2, g=2)
                            for g in range(2):
                                hs = [h for h in range(FIRST[c], FIRST[c] + SPAN) if h // 8 == g]
                                if hs:
                                    i0, n = hs[0] - FIRST[c], len(hs)
                                    dst = v_rows[:, :, b, c, i0 * (HD + 1):(i0 + n) * (HD + 1)].rearrange(
                                        "p w (h d) -> p w h d", d=HD + 1)[:, :, :, 0:HD]
                                    f0 = hs[0] % 8 * HD
                                    ins = e.activation(dst, both[:, :, g, f0:f0 + n * HD].rearrange(
                                        "p w (h d) -> p w h d", d=HD), ACT.Copy)
                            ins.then_inc(read[bk], 1)
                            continue
                        e.activation(w_vo[:, b, c, :], bank[bk][:, 0:D], ACT.Copy,
                                     scale=tg[:, layer:layer + 1]).then_inc(read[bk], 1)
                if kind in ("aX", "fX"):
                    w = 0 if kind == "aX" else 1
                    bk = "T0" if w == 0 else "T1"
                    got(bk)
                    e.activation(xh[:, w, :, :], bank[bk][:, :].rearrange("p (c t) -> p c t", c=KC),
                                 ACT.Copy).then_inc(ev["a_xh" if w == 0 else "f_xh"], 1)
                if kind == "aZ":
                    for o2 in range(2 if layer == 0 else 1):
                        bk = f"T{1 - o2}"
                        got(bk)
                        z = bank[bk][:, :].rearrange("p (c t) -> p c t", c=2)
                        if layer == 0:
                            e.activation(q_t[:, 2 * o2:2 * o2 + 2, :], z, ACT.Exp, scale=1.0 / WS,
                                         bias=consts["fm_b"][:, 0:1]).then_inc(read[bk], 1)
                        else:
                            e.activation(q_t[:, 0, :], z[:, 0, :], ACT.Identity, scale=1.0 / WS,
                                         bias=consts["bq"][:, 0:1])
                            e.activation(q_t[:, 1, :], z[:, 1, :], ACT.Identity, scale=1.0 / WS,
                                         bias=consts["bq"][:, 1:2]).then_inc(read[bk], 1)
                            e.wait_ge(read[bk], t.past(bk, 1))
                            e.activation(q16[:, 0, :, :], q_t[:, 0:2, :], ACT.Copy).then_inc(ev["a_qh"], 1)
                if kind == "aS":
                    u = st[3]
                    s, half = u // 2, u % 2
                    bk = f"S{u % 2}"
                    e.wait_ge(read[bk], t.past(bk, 1))
                    v = probs[:, s, half * 2 * GW:(half + 1) * 2 * GW] if layer == 0 else diff[:, u % 2, :]
                    scale = D ** -0.5 if layer == 0 else HD ** -0.5
                    e.activation(v, v, ACT.Exp, scale=scale).then_inc(ev["a_exp"], 1)
                if kind == "aN" and layer == 1:
                    u = st[3]
                    s, half = u // 2, u % 2
                    e.wait_ge(ev["a_exp"], t.past("a_rs", 1))
                    e.activation(probs16[:, s, 0, half * 2 * GW:(half + 1) * 2 * GW], diff[:, u % 2, :],
                                 ACT.Copy).then_inc(ev["a_rs"], 1)
                if kind == "aQ":
                    got("T1")
                    e.activation(v_t[:, 0, :, :], bank["T1"][:, 0:D].rearrange("p (c t) -> p c t", c=KC),
                                 ACT.Copy).then_inc(ev["a_vh"], 1)
                if kind in ("aT", "aU"):
                    for piece, bk in ((0, "T1"), (1, "T0")) if kind == "aT" else ((2, "T1"),):
                        got(bk)
                        n = min(4, NCH - 4 * piece)
                        if layer == 1:
                            e.activation(probs_t16[:, 4 * piece:4 * piece + n, :, :].rearrange("p c w t -> p (c w t)"),
                                         bank[bk][:, 0:n * P].bitcast(F16), ACT.Copy).then_inc(read[bk], 1)
                            continue
                        e.activation(probs_t[:, 4 * piece:4 * piece + n, :],
                                     bank[bk][:, 0:n * P].rearrange("p (c t) -> p c t", c=n),
                                     ACT.Copy).then_inc(read[bk], 1)
                if kind == "fH":
                    got("T0")
                    e.activation(h_t, bank["T0"][:, 0:TB], ACT.Relu, scale=1.0 / WS,
                                 bias=consts["b1"][:, 0:1]).then_inc(read["T0"], 1)
                if kind == "fB":
                    got("T0")
                    e.activation(one_hot_t[:, :, :], bank["T0"][:, 0:P].bitcast(F16).rearrange(
                        "p (s t) -> p s t", s=SUB), ACT.Copy).then_inc(read["T0"], 1)
                if kind in ("fB", "fE", "fD"):
                    bk = f"F{st[3] % 2}" if kind == "fE" else "T1"
                    slot = 0 if kind == "fB" else st[3] % 2
                    dst = scaled[layer][:, slot, :, :]
                    src = bank[bk][:, :].rearrange("p (s n) -> p s n", s=SUB)
                    got(bk)
                    at_least(e, ev[f"f_add{slot}"], t.past(f"f_add{slot}"))
                    if kind == "fB" or st[3] == E:
                        e.activation(dst, src, ACT.Copy, scale=tgw[:, layer:layer + 1]).then_inc(read[bk], 1)
                    else:
                        e.wait_ge(ev["f_gate"], t.past("f_gate"))
                        for s in range(SUB):
                            ins = e.activation(dst[:, s, :], src[:, s, :], ACT.Copy,
                                               scale=gate[:, s, st[3]:st[3] + 1])
                        ins.then_inc(read[bk], 1)
                if kind == "fR" and st[3] == 1:
                    e.wait_ge(ev["f_nmx"], t.past("f_nmx"))
                    e.activation(expo[:, :, :], shifted[:, :, :], ACT.Exp).then_inc(ev["f_re"], 1)
                if kind == "fG":
                    j = st[3]
                    got(f"F{j % 2}")
                    e.activation(th[:, j % 2, :], bank[f"F{j % 2}"][:, 0:TB], ACT.Tanh,
                                 scale=0.5 / WS).then_inc(ev["f_th"], 1)
                if kind == "fA":
                    j = st[3]
                    bk = f"F{j % 2}"
                    e.wait_ge(read[bk], t.past(bk))
                    e.activation(act[:, 0, j, :], act_f[:, j % 2, :], ACT.Copy).then_inc(ev["f_ah"], 1)

            run(sc, handle, "ACT")

        @block.gpsimd
        def _(pool):
            pool.memset(padded[:, :, :], 0.0)
            pool.memset(probs[:, :, HK:HKP], 0.0)
            pool.memset(one_hot[:, :, :], 0.0)
            pool.memset(eb[0][:, :], 0.0)
            pool.memset(eb[1][:, :], 0.0)
            pool.memset(eps_t[:, :], EPS)
            pool.memset(rs_exp[:, :], -0.5).then_inc(pool_seq, 1)
            pool.wait_ge(pool_seq, 1)

            def handle(e, t, st, blk):
                kind, layer = st[0], st[1]

                def link(ins):
                    ins.then_inc(pool_seq, 1)
                    e.wait_ge(pool_seq, t.past("pool_seq", 2))
                    t.step({"pool_seq": 1})

                if kind in ("aL", "fL"):
                    w = 0 if kind == "aL" else 1
                    pre = "a" if w == 0 else "f"
                    e.wait_ge(ev[pre + "_stats"], t.past(pre + "_stats", 1))
                    link(e.tensor_tensor(rstd[:, w, :], mv[:, w, :, 1], eps_t[:, :], ALU.add))
                    e.tensor_tensor(rstd[:, w, :], rstd[:, w, :], rs_exp[:, :],
                                    ALU.pow).then_inc(ev[pre + "_rstd"], 1)
                if kind in ("fB", "fE", "fD"):
                    bk = f"F{st[3] % 2}" if kind == "fE" else "T1"
                    slot = 0 if kind == "fB" else st[3] % 2
                    e.wait_ge(read[bk], t.past(bk, 1))
                    for i in range(2):
                        at_least(e, ev[f"f_add{i}"], t.past(f"f_add{i}"))
                    e.tensor_tensor(unused_pool[:, :], eps_t[:, 0:1], eps_t[:, 0:1], ALU.add)
                    xs = x_sb[:, bass.ts(blk, SUB), :]
                    e.tensor_tensor(xs, xs, scaled[layer][:, slot, :, :], ALU.add).then_inc(ev[f"f_add{slot}"], 1)
                if kind == "aM":
                    e.wait_ge(ev["a_xn"], t.past("a_xn", 1))
                    xs = x_sb[:, bass.ts(blk, SUB), :]
                    e.tensor_tensor(xs, xs, x_bias[:, layer, :].unsqueeze(1).broadcast_to([P, SUB, D]),
                                    ALU.add).then_inc(ev["a_xb"], 1)
                if kind == "aZ" and layer == 1:
                    e.wait_ge(ev["a_qh"], t.past("a_qh", 1))
                    e.tensor_tensor(q16[:, 1, :, :], q_t[:, 0:2, :], q16[:, 0, :, :],
                                    ALU.subtract).then_inc(ev["a_ql"], 1)
                if kind == "aN" and layer == 1:
                    u = st[3]
                    s, half = u // 2, u % 2
                    e.wait_ge(ev["a_rs"], t.past("a_rs", 1))
                    cols_ = slice(half * 2 * GW, (half + 1) * 2 * GW)
                    e.tensor_tensor(probs16[:, s, 1, cols_], diff[:, u % 2, :], probs16[:, s, 0, cols_],
                                    ALU.subtract).then_inc(ev["a_pn"], 1)
                    return
                if kind == "fA":
                    j = st[3]
                    e.wait_ge(ev["f_ah"], t.past("f_ah", 1))
                    e.tensor_tensor(act[:, 1, j, :], act_f[:, j % 2, :], act[:, 0, j, :],
                                    ALU.subtract).then_inc(ev["f_act"], 1)
                if kind == "aN":
                    u = st[3]
                    s, half = u // 2, u % 2
                    e.wait_ge(ev["a_rs"], t.past("a_rs", 1))
                    v = probs[:, s, half * 2 * GW:(half + 1) * 2 * GW].rearrange("p (h k) -> p h k", k=NK)
                    e.tensor_tensor(v, v, row_inv[:, 1, u % 2, :].unsqueeze(2).broadcast_to([P, 8, NK]),
                                    ALU.mult).then_inc(ev["a_pn"], 1)

            run(pool, handle, "POOL")

        @block.vector
        def _(dve):
            start = Tally()

            def chain(e, t, ins):
                ins.then_inc(dve_seq, 1)
                e.wait_ge(dve_seq, t.past("dve_seq", 1))
                t.step({"dve_seq": 1})

            dve.wait_ge(first_in, 16 * len(first_loads))
            dve.tensor_tensor(
                zw32[:, :, :].rearrange("p a (g e) -> p (a g) e", e=16),
                consts["fm_rep"][:, :].unsqueeze(1).broadcast_to([P, 16, 16]),
                zmask[:, :].rearrange("p (g e) -> p g e", e=16), ALU.mult)
            chain(dve, start, dve.tensor_tensor(consts["fm_b"][:, :], consts["fm_b"][:, :],
                                                consts["sign"][:, :], ALU.mult))
            dve.tensor_copy(unused[:, :], consts["sign"][:, :]).then_inc(ready, 1)
            chain(dve, start, dve.tensor_scalar(zw[0][:, :, :], zw32[:, :, :], WS, None, ALU.mult))
            chain(dve, start, dve.scalar_tensor_tensor(zw[1][:, :, :], zw32[:, :, :], WS, zw[0][:, :, :],
                                                       ALU.mult, ALU.subtract))
            dve.wait_ge(pool_seq, 1)
            dve.wait_ge(small_in, 16 * len(small_loads))
            dve.wait_ge(tanh_done, 1)
            dve.tensor_copy(ident16[:, :], ident[:, :])
            dve.tensor_scalar(
                mask_low[:, :, :].rearrange("p b (h k) -> p b h k", h=4),
                mask_i.unsqueeze(2).broadcast_to([P, B, 4, NK]), 0.0, FINITE_LOW, ALU.is_equal, ALU.mult)
            dve.memset(share[:, :], 1.0 / P)
            dve.tensor_scalar(tgx[:, :], tg[:, 1:2], 1.0 / WS, None, ALU.mult)
            dve.tensor_scalar(tgw[:, :], tg[:, 2:4], 1.0 / WS, None, ALU.mult)
            for layer in range(2):
                ins = dve.tensor_scalar(x_bias[:, layer, :], consts["ob"][:, layer * D:layer * D + D],
                                        tg[:, layer:layer + 1], None, ALU.mult)
            chain(dve, start, ins)
            dve.tensor_copy(unused[:, :], iota8[:, 0:1]).then_inc(ready, 1)
            base = start.n["dve_seq"]

            def handle(e, t, st, blk):
                kind, layer = st[0], st[1]

                def link(ins):
                    ins.then_inc(dve_seq, 1)
                    e.wait_ge(dve_seq, t.past("dve_seq", base + 1))
                    t.step({"dve_seq": 1})

                def settle(e):
                    e.tensor_copy(unused[:, :], iota8[:, 0:1])

                def block_keys(b):
                    head = mask4[:, :].unsqueeze(2).broadcast_to([P, 4, NK])
                    for g in range(4):
                        kf = feat[:, g, b * NK:b * NK + NK].unsqueeze(1).broadcast_to([P, 4, NK])
                        ins = e.tensor_tensor(k_bd[:, b, g * GW:(g + 1) * GW].rearrange("p (h k) -> p h k", k=NK),
                                              kf, head, ALU.mult)
                    return ins

                def got(name, use=0):
                    e.wait_ge(filled[name], t.past(name, use + 1))

                def mine(name, use=0):
                    e.wait_ge(read[name], t.past(name, use + 1))

                if kind == "split":
                    k = st[3]
                    src, hi, lo = pieces[k]
                    e.wait_ge(split_hi, k + 1)
                    np_ = src.shape[0]
                    e.scalar_tensor_tensor(lo[0:np_], staged(k, hi)[0:np_], WS, hi[0:np_], ALU.mult,
                                           ALU.subtract).then_inc(split_lo, 1)
                if kind == "loaded" and st[3] == 0:
                    e.wait_ge(x_in, 16 * (B // 2))
                    settle(e)
                if kind == "pC":
                    e.memset(zero16, 0.0)
                    e.memset(padded16[:, :, :, :], 0.0)
                    for b in range(B):
                        ones = v_rows[:, :, b, :, :].rearrange("p w c (h d) -> p w c h d", h=SPAN)
                        e.tensor_copy(ones[:, 0, :, :, HD], consts["owner"][:, :].rearrange(
                            "p (c h) -> p c h", c=NCH))
                        e.memset(ones[:, 1, :, :, HD], 0.0)
                    for g in range(4):
                        ins = e.tensor_copy(feat16[:, 0, g, :], feat1[g])
                    link(ins)
                    for g in range(4):
                        ins = e.tensor_tensor(feat16[:, 1, g, :], feat1[g], feat16[:, 0, g, :], ALU.subtract)
                    link(ins)
                if kind == "pK":
                    for b in range(1, B):
                        ins = block_keys(b)
                    link(ins)
                if kind == "pZ":
                    link(e.memset(probs16[:, :, 0, HK:HKP], 0.0))
                if kind == "pV":
                    b = st[3]
                    if layer == 0 and b == 0:
                        e.wait_ge(read["T0"], t.past("T0"))
                        e.wait_ge(read["T1"], t.past("T1"))
                    if b > 0:
                        e.wait_ge(filled["T1"], t.past("T1"))
                        e.wait_ge(filled["T0"], t.past("T0"))
                    keys = slice(b * NK, b * NK + NK)
                    if layer == 0:
                        if b == 0:
                            link(block_keys(b))
                        last = e.tensor_copy(padded[:, :, P:P + GW],
                                             k_bd[:, b, :].rearrange("p (g c) -> p g c", g=4))
                    else:
                        head = mask8[:, :].unsqueeze(2).broadcast_to([P, 8, NK])
                        for w in range(2):
                            for g in range(2):
                                e.tensor_tensor(
                                    k16[:, b, w, g * 2 * GW:(g + 1) * 2 * GW].rearrange("p (h k) -> p h k", k=NK),
                                    feat16[:, w, g, keys].unsqueeze(1).broadcast_to([P, 8, NK]), head, ALU.mult)
                                last = e.tensor_tensor(
                                    padded16[:, w, g, P:P + 2 * GW].rearrange("p (h k) -> p h k", k=NK),
                                    feat16[:, w, 2 + g, keys].unsqueeze(1).broadcast_to([P, 8, NK]), head,
                                    ALU.mult)
                    last.then_inc(ev["p_kv"], 1)
                if kind in ("aL", "fL"):
                    w = 0 if kind == "aL" else 1
                    pre = "a" if w == 0 else "f"
                    if w == 0 and layer == 0 and t.it is not None:
                        e.wait_ge(x_late_in, 16 * (B // 2))
                    if w == 0 and layer == 1:
                        for i in range(2):
                            e.wait_ge(ev[f"f_add{i}"], t.past(f"f_add{i}", -(E // 2 + 1 - i)))
                    if w == 1:
                        at_least(e, read["T0"], t.past("T0"))
                    for s in range(SUB):
                        ins = e.bn_stats(stats[:, w, s, :], x_sb[:, blk * SUB + s, :])
                    link(ins)
                    settle(e)
                    for s in range(SUB):
                        ins = e.bn_aggr(mv[:, w, s, :], stats[:, w, s, :])
                    ins.then_inc(ev[pre + "_stats"], 1)
                if kind in ("aM", "fN"):
                    w = 0 if kind == "aM" else 1
                    pre = "a" if w == 0 else "f"
                    at_least(e, ev[pre + "_xh"], t.past(pre + "_xh"))
                    e.wait_ge(ev[pre + "_rstd"], t.past(pre + "_rstd"))
                    for s in range(SUB):
                        ins = e.tensor_scalar(xn[:, w, s, :], x_sb[:, blk * SUB + s, :], mv[:, w, s, 0:1],
                                              rstd[:, w, s:s + 1], ALU.subtract, ALU.mult)
                    ins.then_inc(ev[pre + "_xn"], 1)
                if kind in ("aX", "fX"):
                    w = 0 if kind == "aX" else 1
                    bk, evn = ("T0", "a_xh") if w == 0 else ("T1", "f_xh")
                    e.wait_ge(ev[evn], t.past(evn, 1))
                    e.tensor_tensor(xl[:, w, :, :], bank[bk][:, :].rearrange("p (c t) -> p c t", c=KC),
                                    xh[:, w, :, :], ALU.subtract).then_inc(read[bk], 1)
                if kind == "aS":
                    u = st[3]
                    s, half = u // 2, u % 2
                    bk = f"S{u % 2}"
                    got(bk)
                    sc_ = bank[bk][:, :, 0:GW].rearrange("p g (h k) -> p g h k", k=NK)
                    v = probs[:, s, half * 2 * GW:(half + 1) * 2 * GW] if layer == 0 else diff[:, u % 2, :]
                    if layer == 1:
                        e.wait_ge(ev["a_pn"], t.past("a_pn"))
                    v4 = v.rearrange("p (g h k) -> p g h k", g=2, k=NK)
                    m = row_max[:, u % 2, :]
                    link(e.tensor_reduce(m.rearrange("p (g h) -> p g h", g=2), sc_, AX, ALU.max))
                    mb = m.rearrange("p (g h) -> p g h", g=2).unsqueeze(3).broadcast_to([P, 2, 4, NK])
                    e.tensor_tensor(v4, sc_, mb, ALU.subtract).then_inc(read[bk], 1)
                if kind == "aN" and layer == 0:
                    u = st[3]
                    s, half = u // 2, u % 2
                    e.wait_ge(ev["a_exp"], t.past("a_rs", 1))
                    v = probs[:, s, half * 2 * GW:(half + 1) * 2 * GW].rearrange("p (h k) -> p h k", k=NK)
                    if u >= 2:
                        e.wait_ge(ev["a_pn"], t.past("a_pn", -1))
                    link(e.tensor_reduce(row_inv[:, 0, u % 2, :], v, AX, ALU.add))
                    e.reciprocal(row_inv[:, 1, u % 2, :], row_inv[:, 0, u % 2, :]).then_inc(ev["a_rs"], 1)
                if kind == "aO":
                    s = st[3]
                    got("T0")
                    e.wait_ge(ev["a_xb"], t.past("a_xb"))
                    xs = x_sb[:, blk * SUB + s, :]
                    if layer == 0:
                        e.tensor_tensor(xs, bank["T0"][:, 0:D], xs, ALU.add).then_inc(read["T0"], 1)
                    else:
                        e.scalar_tensor_tensor(xs, bank["T0"][:, 0:D], tgx[:, 0:1], xs, ALU.mult,
                                               ALU.add).then_inc(read["T0"], 1)
                if kind == "aP":
                    s = st[3]
                    got("T0")
                    o = bank["T0"][:, 0:H * (HD + 1)].rearrange("p (h d) -> p h d", h=H)
                    link(e.reciprocal(head_inv[:, :], o[:, :, HD]))
                    e.tensor_tensor(probs[:, s, 0:D].rearrange("p (h d) -> p h d", h=H), o[:, :, 0:HD],
                                    head_inv[:, :].unsqueeze(2).broadcast_to([P, H, HD]),
                                    ALU.mult).then_inc(read["T0"], 1)
                if kind == "aQ":
                    e.wait_ge(ev["a_vh"], t.past("a_vh", 1))
                    e.tensor_tensor(v_t[:, 1, :, :], bank["T1"][:, 0:D].rearrange("p (c t) -> p c t", c=KC),
                                    v_t[:, 0, :, :], ALU.subtract).then_inc(read["T1"], 1)
                if kind == "fH":
                    e.wait_ge(read["T0"], t.past("T0", 1))
                    link(e.tensor_copy(h_hi[:, :], h_t))
                    e.tensor_tensor(h_lo[:, :], h_t, h_hi[:, :], ALU.subtract).then_inc(ev["f_hs"], 1)
                if kind == "fM":
                    got("T1")
                    link(e.scalar_tensor_tensor(
                        logits[:, :, :], bank["T1"][:, 0:SUB * E].rearrange("p (s e) -> p s e", e=E), 1.0 / WS,
                        consts["b2"][:, :].unsqueeze(1).broadcast_to([P, SUB, E]), ALU.mult, ALU.add))
                    settle(e)
                    for s in range(SUB):
                        ins = e.max(top[:, s, :], logits[:, s, :])
                    link(ins)
                    settle(e)
                    for s in range(SUB):
                        ins = e.max_index(idx[:, s, :], top[:, s, :], logits[:, s, :])
                    link(ins)
                    link(e.tensor_copy(rank[:, :, :], idx[:, :, :]))
                    for i in range(2):
                        at_least(e, read[f"F{i}"], t.past(f"F{i}"))
                    for s in range(SUB):
                        ins = e.tensor_scalar(gate[:, s, :], iota8[:, :], rank[:, s, 0:1], tgw[:, 0:1],
                                              ALU.is_equal, ALU.mult)
                    ins.then_inc(ev["f_gate"], 1)
                    for s in range(SUB):
                        e.tensor_scalar(one_hot[:, s, 0:E], iota8[:, :], rank[:, s, 0:1], None, ALU.is_equal)
                    e.tensor_copy(unused[:, :], iota8[:, 0:1]).then_inc(read["T1"], 1)
                if kind == "fR":
                    def wide(col):
                        return col.broadcast_to([P, SUB, E])

                    if st[3] == 0:
                        got("T0")
                        e.tensor_scalar(logits[:, :, :], bank["T0"][:, 0:SUB * E].rearrange(
                            "p (s e) -> p s e", e=E), 1.0 / WS, None, ALU.mult).then_inc(read["T0"], 1)
                        mine("T0")
                        settle(e)
                        for s in range(SUB):
                            ins = e.max(top[:, s, :], logits[:, s, :])
                        link(ins)
                        e.tensor_tensor(shifted[:, :, :], logits[:, :, :], wide(top[:, :, 0:1]),
                                        ALU.subtract).then_inc(ev["f_nmx"], 1)
                    if st[3] == 2:
                        e.wait_ge(ev["f_re"], t.past("f_re"))
                        link(e.tensor_reduce(total[:, 0, :], expo[:, :, :], AX, ALU.add))
                        link(e.reciprocal(total[:, 1, :], total[:, 0, :]))
                        link(e.tensor_tensor(score[:, :, :], expo[:, :, :], wide(total[:, 1, :].unsqueeze(2)),
                                             ALU.mult))
                        link(e.tensor_scalar(corrected[:, :, :], score[:, :, :], consts["rb"][:, 0:1], None,
                                             ALU.add))
                        settle(e)
                        for s in range(SUB):
                            ins = e.max(top[:, s, :], corrected[:, s, :])
                        link(ins)
                        settle(e)
                        for s in range(SUB):
                            ins = e.max_index(idx[:, s, :], top[:, s, :], corrected[:, s, :])
                        link(ins)
                        link(e.tensor_copy(rank[:, :, :], idx[:, :, :]))
                    if st[3] == 3:
                        for s in range(SUB):
                            ins = e.tensor_tensor(match[:, s, :, :],
                                                  iota8[:, :].unsqueeze(2).broadcast_to([P, E, TOPK]),
                                                  rank[:, s, 0:TOPK].unsqueeze(1).broadcast_to([P, E, TOPK]),
                                                  ALU.is_equal)
                        link(ins)
                        link(e.tensor_reduce(chosen[:, :, :], match[:, :, :, :], AX, ALU.add))
                        link(e.tensor_tensor(kept[:, :, :], score[:, :, :], chosen[:, :, :], ALU.mult))
                        link(e.tensor_reduce(total[:, 2, :], kept[:, :, :], AX, ALU.add))
                        link(e.tensor_scalar(total[:, 2, :], total[:, 2, :], 1e-20, None, ALU.add))
                        link(e.reciprocal(total[:, 3, :], total[:, 2, :]))
                        at_least(e, read["T1"], t.past("T1"))
                        e.scalar_tensor_tensor(gate[:, :, :], kept[:, :, :], tgw[:, 1:2],
                                               wide(total[:, 3, :].unsqueeze(2)), ALU.mult,
                                               ALU.mult).then_inc(ev["f_gate"], 1)
                if kind == "fA":
                    j = st[3]
                    n = t.past("f_act", 1)
                    bk = f"F{j % 2}"
                    e.wait_ge(ev["f_th"], n)
                    at_least(e, ev["f_act"], t.past("f_act", -1))
                    link(e.scalar_tensor_tensor(th[:, j % 2, :], th[:, j % 2, :], 1.0, bank[bk][:, 0:TB],
                                                ALU.add, ALU.mult))
                    e.scalar_tensor_tensor(act_f[:, j % 2, :], th[:, j % 2, :], 0.5 / WS / WS,
                                           bank[bk][:, TB:2 * TB], ALU.mult, ALU.mult).then_inc(read[bk], 1)

            run(dve, handle, "DVE")


CONSTS = {"zmask": (256,), "fm_rep": (16,), "fm_b": (1,), "sign": (1,), "g_all": (4,), "ident": (P,), "mask4": (4,), "mask8": (8,), "owner": (NCH * SPAN,), "iota8": (E,),
          "b1": (1,), "b2": (E,), "bq": (KC,),
          "bkv": (2 * KC,), "rb": (1,), "ob": (2 * D,)}


def kernel(**inputs):
    import concourse.bacc as bacc
    from concourse.bass_utils import run_bass_kernel_spmd

    f = {k: np.ascontiguousarray(v) for k, v in inputs.items()}

    def rows(v):
        return np.ascontiguousarray(np.broadcast_to(v.reshape(1, -1), (P, v.size)))

    def cols(v):
        return np.ascontiguousarray(v.reshape(-1, P).T)

    p = np.arange(P)
    zmask = np.zeros((P, 2, 4, 2, 16), np.float32)
    for q in range(P):
        h = q // 16
        zmask[q, h // 4, h % 4, 0, :] = 1.0
        zmask[q, h // 4, h % 4, 1, :] = -1.0
    row = P * np.arange(NCH)[:, None] + p
    owner = (row // NK).T[:, :, None] == (np.array(FIRST)[:, None] + np.arange(SPAN))[None]
    arrays = {
        "x": f["x"], "ctxT": np.ascontiguousarray(f["ctx_1024"].reshape(B * NK, D).T),
        "WqT": np.ascontiguousarray(f["L1_xattn_Wq"].T), "WkT": np.ascontiguousarray(f["L1_xattn_Wk"].T),
        "WvT": np.ascontiguousarray(f["L1_xattn_Wv"].T), "WoT": np.ascontiguousarray(f["L1_xattn_Wo"].T),
        "fcT": np.ascontiguousarray(f["L0_xattn_fc_w"].T), "expert_b": f["L0_ffn_expert_b"],
        "mask": rows(f["mask_BxS2_ik0"].astype(np.int32)).reshape(P, B, NK),
        "ident": np.eye(P, dtype=np.float32), "zmask": zmask.reshape(P, 256),
        "mask4": (p[:, None] // 32 == np.arange(4)).astype(np.float32),
        "mask8": (p[:, None] // 16 == np.arange(8)).astype(np.float32),
        "owner": owner.reshape(P, NCH * SPAN).astype(np.float32),
        "iota8": rows(np.arange(E, dtype=np.float32)),
        "g_all": rows(np.concatenate([f["g_xattn"], f["g_ffn"]])),
        "fm_rep": np.ascontiguousarray(np.tile(f["L0_xattn_fm_w"].T, (8, 1))), "fm_b": np.tile(f["L0_xattn_fm_b"], 8).reshape(P, 1),
        "sign": np.where(p % 32 < 16, 1.0, -1.0).astype(np.float32).reshape(P, 1),
        "b1": cols(f["L0_ffn_b1"]), "b2": rows(f["L0_ffn_b2"]), "bq": cols(f["L1_xattn_bq"]),
        "bkv": np.concatenate([cols(f["L1_xattn_bk"]), cols(f["L1_xattn_bv"])], axis=1),
        "rb": rows(f["L1_ffn_router_bias"].reshape(1)),
        "ob": rows(np.concatenate([f["L0_xattn_fc_b"], f["L1_xattn_bo"]])),
    }
    for n in ("L0_ffn_W1", "L0_ffn_W2", "L0_ffn_expert_W", "L1_ffn_router_w", "L1_ffn_gate_w", "L1_ffn_up_w",
              "L1_ffn_down_w", "L1_ffn_s_gate_w", "L1_ffn_s_up_w", "L1_ffn_s_down_w"):
        arrays[n] = f[n]
    nc = bacc.Bacc("TRN2", target_bir_lowering=False, num_devices=1)
    args = {}
    for n, v in arrays.items():
        v = arrays[n] = np.ascontiguousarray(v)
        args[n] = nc.dram_tensor("in_" + n, v.shape, mybir.dt.from_np(v.dtype), kind="ExternalInput").ap()
    args["out"] = nc.dram_tensor("out_x", (B * S, D), F32, kind="ExternalOutput").ap()
    gated_layers(nc, args)
    got = run_bass_kernel_spmd(nc, [{"in_" + n: v for n, v in arrays.items()}], core_ids=[0])
    return got.results[0]["out_x"].reshape(B, S, D)
```
